# Optimizing a Trainium2 kernel written in Bass

```python
import numpy as np
import jax
import jax.numpy as jnp

def _softmax(x, axis=-1):
    return jax.nn.softmax(x, axis=axis)

def _gelu(x):
    return jax.nn.gelu(x, approximate=True)

def _silu(x):
    return jax.nn.silu(x)

def _sigmoid(x):
    return jax.nn.sigmoid(x)

def _layernorm(x, axis=-1, eps=1e-05):
    m = jnp.mean(x, axis=axis, keepdims=True)
    v = jnp.var(x, axis=axis, keepdims=True)
    return (x - m) / jnp.sqrt(v + eps)

def _scatter_add(tgt, idx, src, axis=0):
    return tgt.at[idx].add(src)

def _segment_sum(src, seg, n):
    return jax.ops.segment_sum(src, seg, n)
kernel_name = 'mk_cond_seq_d2_seqx_r8_811a5c'

def setup_inputs(seed: int=0):
    np.random.seed(seed)
    _w = jnp.asarray

    def _rec_inputs():
        import jax
        import jax.numpy as jnp
        _rk = jax.random.key(seed)
        x = -0.0003929 + 0.9999 * jax.random.normal(jax.random.fold_in(_rk, 1), (8, 128, 256), jnp.float32)
        _lenS = 128 - jax.random.randint(jax.random.fold_in(_rk, 7), (8,), 0, max(1, 128 // 4) + 1, jnp.int32)
        _lenS2 = 128 - jax.random.randint(jax.random.fold_in(_rk, 8), (8,), 0, max(1, 128 // 4) + 1, jnp.int32)
        pos_BxS = jnp.broadcast_to(jnp.arange(128, dtype=jnp.int32), (8, 128))
        cond_2048 = 0.00782532 + 1.00527 * jax.random.normal(jax.random.fold_in(_rk, 12), (8, 256), jnp.float32)
        return (x, pos_BxS, cond_2048)
    x, pos_BxS, cond_2048 = _rec_inputs()

    def _L0_cond_setup():
        import jax, jax.numpy as jnp
        import numpy as np
        HIDDEN, NQ, NKV, HD, INTER = (256, 8, 1, 32, 1024)
        B, S = (4, 256)
        EPS = 1e-06
        ROPE_BASE = 10000.0

        def ada_rms(x, t, w, tw):
            n = x * jax.lax.rsqrt(jnp.mean(jnp.square(x), axis=-1, keepdims=True) + EPS)
            scale = t @ tw.T
            return n * (w * (1.0 + scale))[:, None, :]

        def apply_rope(x, pos_ids):
            half = HD // 2
            inv_freq = 1.0 / ROPE_BASE ** (jnp.arange(0, HD, 2, dtype=jnp.float32) / HD)
            ang = pos_ids.astype(jnp.float32)[:, :, None] * inv_freq
            cos = jnp.concatenate([jnp.cos(ang), jnp.cos(ang)], axis=-1)[:, None]
            sin = jnp.concatenate([jnp.sin(ang), jnp.sin(ang)], axis=-1)[:, None]
            x1, x2 = (x[..., :half], x[..., half:])
            rot = jnp.concatenate([-x2, x1], axis=-1)
            return x * cos + rot * sin
        key = jax.random.key(seed)
        ks = jax.random.split(key, 12)
        f32 = jnp.float32
        inp = {'x': jax.random.normal(ks[0], (B, S, HIDDEN), f32), 'pos_ids': jnp.broadcast_to(jnp.arange(S, dtype=jnp.int32), (B, S)), 'time_emb': jax.random.normal(ks[1], (B, HIDDEN), f32), 'ln1_w': jnp.ones((HIDDEN,), f32), 'ln1_tw': jax.random.normal(ks[2], (HIDDEN, HIDDEN), f32) * 0.02, 'ln2_w': jnp.ones((HIDDEN,), f32), 'ln2_tw': jax.random.normal(ks[3], (HIDDEN, HIDDEN), f32) * 0.02, 'Wq': jax.random.normal(ks[4], (NQ * HD, HIDDEN), f32) * 0.02, 'Wk': jax.random.normal(ks[5], (NKV * HD, HIDDEN), f32) * 0.02, 'Wv': jax.random.normal(ks[6], (NKV * HD, HIDDEN), f32) * 0.02, 'Wo': jax.random.normal(ks[7], (HIDDEN, NQ * HD), f32) * 0.02, 'Wg': jax.random.normal(ks[8], (INTER, HIDDEN), f32) * 0.02, 'Wu': jax.random.normal(ks[9], (INTER, HIDDEN), f32) * 0.02, 'Wd': jax.random.normal(ks[10], (HIDDEN, INTER), f32) * 0.02}
        return inp
    _L0_cond_all = _L0_cond_setup()
    _L0_cond_in = {k: v for k, v in _L0_cond_all.items() if k in ('ln1_w', 'ln1_tw', 'ln2_w', 'ln2_tw', 'Wq', 'Wk', 'Wv', 'Wo', 'Wg', 'Wu', 'Wd')}
    del _L0_cond_all

    def _L1_cond_setup():
        import jax, jax.numpy as jnp
        import numpy as np
        B, T, LATENT, FFN, TEMB = (4, 512, 32, 128, 256)
        D = 8 * LATENT
        LN_EPS = 1e-05

        def _layernorm(h, g, b):
            mu = jnp.mean(h, axis=-1, keepdims=True)
            var = jnp.mean(jnp.square(h - mu), axis=-1, keepdims=True)
            return (h - mu) * jax.lax.rsqrt(var + LN_EPS) * g + b
        key = jax.random.key(seed)
        ks = jax.random.split(key, 12)
        s1 = 1.0 / np.sqrt(LATENT)
        s2 = 1.0 / np.sqrt(FFN)
        sd = 1.0 / np.sqrt(D)
        st = 1.0 / np.sqrt(TEMB)
        return {'x': jax.random.normal(ks[0], (B, T, D), dtype=jnp.float32), 'emb': jax.random.normal(ks[1], (B, TEMB), dtype=jnp.float32), 'W1': jax.random.uniform(ks[2], (8, LATENT, FFN), jnp.float32, -s1, s1), 'b1': jax.random.uniform(ks[3], (8, FFN), jnp.float32, -s1, s1), 'W2': jax.random.uniform(ks[4], (8, FFN, LATENT), jnp.float32, -s2, s2), 'b2': jax.random.uniform(ks[5], (8, LATENT), jnp.float32, -s2, s2), 'emb_W': jax.random.uniform(ks[6], (TEMB, 2 * D), jnp.float32, -st, st), 'emb_b': jax.random.uniform(ks[7], (2 * D,), jnp.float32, -st, st), 'ln_g': jnp.ones((D,), jnp.float32), 'ln_b': jnp.zeros((D,), jnp.float32), 'out_W': jax.random.uniform(ks[8], (D, D), jnp.float32, -sd, sd), 'out_b': jax.random.uniform(ks[9], (D,), jnp.float32, -sd, sd)}
    _L1_cond_all = _L1_cond_setup()
    _L1_cond_in = {k: v for k, v in _L1_cond_all.items() if k in ('W1', 'b1', 'W2', 'b2', 'emb_W', 'emb_b', 'ln_g', 'ln_b', 'out_W', 'out_b')}
    del _L1_cond_all
    return {'x': x, 'pos_BxS': pos_BxS, 'cond_2048': cond_2048, 'L0_cond_ln1_w': _L0_cond_in['ln1_w'], 'L0_cond_ln1_tw': _L0_cond_in['ln1_tw'], 'L0_cond_ln2_w': _L0_cond_in['ln2_w'], 'L0_cond_ln2_tw': _L0_cond_in['ln2_tw'], 'L0_cond_Wq': _L0_cond_in['Wq'], 'L0_cond_Wk': _L0_cond_in['Wk'], 'L0_cond_Wv': _L0_cond_in['Wv'], 'L0_cond_Wo': _L0_cond_in['Wo'], 'L0_cond_Wg': _L0_cond_in['Wg'], 'L0_cond_Wu': _L0_cond_in['Wu'], 'L0_cond_Wd': _L0_cond_in['Wd'], 'L1_cond_W1': _L1_cond_in['W1'], 'L1_cond_b1': _L1_cond_in['b1'], 'L1_cond_W2': _L1_cond_in['W2'], 'L1_cond_b2': _L1_cond_in['b2'], 'L1_cond_emb_W': _L1_cond_in['emb_W'], 'L1_cond_emb_b': _L1_cond_in['emb_b'], 'L1_cond_ln_g': _L1_cond_in['ln_g'], 'L1_cond_ln_b': _L1_cond_in['ln_b'], 'L1_cond_out_W': _L1_cond_in['out_W'], 'L1_cond_out_b': _L1_cond_in['out_b']}

def reference(x, pos_BxS, cond_2048, L0_cond_ln1_w, L0_cond_ln1_tw, L0_cond_ln2_w, L0_cond_ln2_tw, L0_cond_Wq, L0_cond_Wk, L0_cond_Wv, L0_cond_Wo, L0_cond_Wg, L0_cond_Wu, L0_cond_Wd, L1_cond_W1, L1_cond_b1, L1_cond_W2, L1_cond_b2, L1_cond_emb_W, L1_cond_emb_b, L1_cond_ln_g, L1_cond_ln_b, L1_cond_out_W, L1_cond_out_b):
    import jax
    import jax.numpy as jnp

    def _L0_cond_ref(x, pos_ids, time_emb, ln1_w, ln1_tw, ln2_w, ln2_tw, Wq, Wk, Wv, Wo, Wg, Wu, Wd):
        import jax, jax.numpy as jnp
        import numpy as np
        HIDDEN, NQ, NKV, HD, INTER = (256, 8, 1, 32, 1024)
        B, S = (4, 256)
        EPS = 1e-06
        ROPE_BASE = 10000.0

        def ada_rms(x, t, w, tw):
            n = x * jax.lax.rsqrt(jnp.mean(jnp.square(x), axis=-1, keepdims=True) + EPS)
            scale = t @ tw.T
            return n * (w * (1.0 + scale))[:, None, :]

        def apply_rope(x, pos_ids):
            half = HD // 2
            inv_freq = 1.0 / ROPE_BASE ** (jnp.arange(0, HD, 2, dtype=jnp.float32) / HD)
            ang = pos_ids.astype(jnp.float32)[:, :, None] * inv_freq
            cos = jnp.concatenate([jnp.cos(ang), jnp.cos(ang)], axis=-1)[:, None]
            sin = jnp.concatenate([jnp.sin(ang), jnp.sin(ang)], axis=-1)[:, None]
            x1, x2 = (x[..., :half], x[..., half:])
            rot = jnp.concatenate([-x2, x1], axis=-1)
            return x * cos + rot * sin
        b, s, _ = x.shape
        g = NQ // NKV
        res = x
        h = ada_rms(x, time_emb, ln1_w, ln1_tw)
        q = (h @ Wq.T).reshape(b, s, NQ, HD).transpose(0, 2, 1, 3)
        k = (h @ Wk.T).reshape(b, s, NKV, HD).transpose(0, 2, 1, 3)
        v = (h @ Wv.T).reshape(b, s, NKV, HD).transpose(0, 2, 1, 3)
        q = apply_rope(q, pos_ids)
        k = apply_rope(k, pos_ids)
        qg = q.reshape(b, NKV, g, s, HD)
        scores = jnp.einsum('bkgsd,bktd->bkgst', qg, k) / jnp.sqrt(jnp.float32(HD))
        attn = jax.nn.softmax(scores, axis=-1)
        ctx = jnp.einsum('bkgst,bktd->bkgsd', attn, v)
        ctx = ctx.reshape(b, NQ, s, HD).transpose(0, 2, 1, 3).reshape(b, s, NQ * HD)
        x = res + ctx @ Wo.T
        res = x
        h = ada_rms(x, time_emb, ln2_w, ln2_tw)
        mlp = jax.nn.silu(h @ Wg.T) * (h @ Wu.T) @ Wd.T
        return res + mlp

    def _L1_cond_ref(x, emb, W1, b1, W2, b2, emb_W, emb_b, ln_g, ln_b, out_W, out_b):
        import jax, jax.numpy as jnp
        import numpy as np
        B, T, LATENT, FFN, TEMB = (4, 512, 32, 128, 256)
        D = 8 * LATENT
        LN_EPS = 1e-05

        def _layernorm(h, g, b):
            mu = jnp.mean(h, axis=-1, keepdims=True)
            var = jnp.mean(jnp.square(h - mu), axis=-1, keepdims=True)
            return (h - mu) * jax.lax.rsqrt(var + LN_EPS) * g + b
        Bx, Tx, Dx = x.shape
        xr = x.reshape(Bx, Tx, 8, LATENT)
        h = jnp.einsum('btel,elf->btef', xr, W1) + b1
        h = jax.nn.gelu(h, approximate=False)
        y = jnp.einsum('btef,efl->btel', h, W2) + b2
        y = y.reshape(Bx, Tx, Dx)
        eo = jax.nn.silu(emb) @ emb_W + emb_b
        scale, shift = jnp.split(eo[:, None, :], 2, axis=-1)
        hn = _layernorm(y, ln_g, ln_b) * (1.0 + scale) + shift
        proj = jax.nn.silu(hn) @ out_W + out_b
        return x + proj
    x = _L0_cond_ref(x, pos_BxS, cond_2048, L0_cond_ln1_w, L0_cond_ln1_tw, L0_cond_ln2_w, L0_cond_ln2_tw, L0_cond_Wq, L0_cond_Wk, L0_cond_Wv, L0_cond_Wo, L0_cond_Wg, L0_cond_Wu, L0_cond_Wd)
    x = _L1_cond_ref(x, cond_2048, L1_cond_W1, L1_cond_b1, L1_cond_W2, L1_cond_b2, L1_cond_emb_W, L1_cond_emb_b, L1_cond_ln_g, L1_cond_ln_b, L1_cond_out_W, L1_cond_out_b)
    return x

_drawn_inputs = setup_inputs


def setup_inputs(seed=0):
    import zlib

    import numpy as np

    out = dict(_drawn_inputs(seed))
    spreads = {'L0_cond_ln1_w': (1.0, 0.6),
     'L0_cond_ln2_w': (1.0, 0.6),
     'L1_cond_ln_g': (1.0, 0.6),
     'L1_cond_ln_b': (0.0, 2.0)}
    factors = {'L0_cond_ln1_tw': 8.0,
     'L0_cond_ln2_tw': 19.395,
     'L0_cond_Wq': 8.0,
     'L0_cond_Wk': 8.0,
     'L0_cond_Wv': 5.596,
     'L0_cond_Wo': 5.651,
     'L1_cond_emb_b': 195.84,
     'L0_cond_Wg': 5.73,
     'L0_cond_Wu': 5.5,
     'L0_cond_Wd': 5.503,
     'L1_cond_W1': 21.68,
     'L1_cond_b1': 64.0,
     'L1_cond_b2': 64.0,
     'L1_cond_emb_W': 35.736,
     'L1_cond_out_b': 64.0,
     'L1_cond_W2': 8.0,
     'L1_cond_out_W': 8.0}
    for name, (base, spread) in spreads.items():
        noise = np.random.default_rng([zlib.crc32(name.encode()), seed]).standard_normal(out[name].shape)
        drawn = base * np.exp(spread * noise) if base else spread * noise
        out[name] = jnp.asarray(drawn.astype(out[name].dtype))
    for name, factor in factors.items():
        out[name] = (out[name] * factor).astype(out[name].dtype)
    return out
```

```python
from contextlib import ExitStack

import concourse.bass as bass
from concourse import mybir

F32 = mybir.dt.float32
F32R = mybir.dt.float32r
BF16 = mybir.dt.bfloat16
I32 = mybir.dt.int32
ALU = mybir.AluOpType
ACT = mybir.ActivationFunctionType
AX = mybir.AxisListType

P = 128
B, S, H = 8, 128, 256
T = B * S
K = H // P
NH, HD = 8, 32
QK = (NH + 1) * HD
QKV = QK + HD
FR = HD // 2
INTER = 1024
FT = INTER // P
E, LAT, FFN = 8, 32, 128
NB = 4
HT = NB * S
HALVES = B // NB
HG = 4
RMS_EPS, LN_EPS = 1e-6, 1e-5
PI = 3.14159265358979
MAGIC = 1.5 * 2.0 ** 23
TAU_A = 6.28125
TAU_B = 1.934051513671875e-3
TAU_C = 2 * PI - TAU_A - TAU_B

RAW_TILES = 4
TABLE_READY = 10

C_LN1W, C_LN2W, C_LNG, C_LNB, C_OUTB, C_B2, C_EMBB, C_B1, C_COND, C_INVF, C_END = (
    0, 2, 4, 6, 8, 10, 12, 16, 24, 40, 56)


def cond_block_kernel(nc, xT, xn, small, posT, ident, tw1, tw2, wqkv, wo, wgu, wd, w1, w2, embw, outw, out):
    ctx = ExitStack()
    with ctx:
        def sb(name, shape, dt=F32):
            return ctx.enter_context(nc.sbuf_tensor(name, shape, dt))

        def sem(name):
            return ctx.enter_context(nc.semaphore(name))

        res_sb = sb("res_sb", [P, K, T])
        xn_sb = sb("xn_sb", [P, B, H])
        small_sb = sb("small_sb", [P, C_END])
        pos_sb = sb("pos_sb", [P, B], I32)
        id_sb = sb("id_sb", [P, P])
        tw_sb = sb("tw_sb", [P, 2, K, H])
        tw1_sb, tw2_sb = tw_sb[:, 0], tw_sb[:, 1]
        emb_sb = sb("emb_sb", [P, K, 2 * H])
        w2_sb = sb("w2_sb", [P, E, LAT])
        sq_raw = sb("sq_raw", [P, K, H])
        wgu_raw = sb("wgu_raw", [P, RAW_TILES, 2, K, P])
        wd_raw = sb("wd_raw", [P, FT, H])
        w1_raw = tw_sb[:].rearrange("p n k h -> p (n k h)").rearrange("p (e f) -> p e f", e=E)
        early = sb("early", [P, 2 * E * FFN], F32R)
        wqkv_hi = early[:, 0:K * QKV].rearrange("p (k m) -> p k m", k=K)
        wqkv_lo = early[:, K * QKV:2 * K * QKV].rearrange("p (k m) -> p k m", k=K)
        xg_lo = early[:, 2 * K * QKV:2 * K * QKV + 3 * K * S].rearrange("p (r k s) -> p r k s", r=3, k=K)
        wo_hi, wo_lo = sb("wo_hi", [P, K, H], F32R), sb("wo_lo", [P, K, H], F32R)
        wgu_hi, wgu_lo = sb("wgu_hi", [P, FT, 2, K, P], F32R), sb("wgu_lo", [P, FT, 2, K, P], F32R)
        wd_hi, wd_lo = sb("wd_hi", [P, FT, H], F32R), sb("wd_lo", [P, FT, H], F32R)
        w1_hi, w1_lo = (early[:, c * E * FFN:(c + 1) * E * FFN].rearrange("p (e f) -> p e f", e=E) for c in range(2))
        outw_hi, outw_lo = sb("outw_hi", [P, K, H], F32R), sb("outw_lo", [P, K, H], F32R)
        negid = sb("negid", [P, P], BF16)
        avg = sb("avg", [P, P])
        ones = sb("ones", [P, HD])
        gain1 = sb("gain1", [P, K, B])
        gain2 = sb("gain2", [P, K, B])
        scond = sb("scond", [P, K, B])
        eps_sb = sb("eps_sb", [P, 2])
        shiftb = sb("shiftb", [P, 2 * K, B])
        lnA = sb("lnA", [P, K, B])
        lnB = sb("lnB", [P, K, B])
        posf = sb("posf", [P, B])
        ang = sb("ang", [P, B * FR])
        prob = sb("prob", [P, 2, NH, S])
        first = prob[:].rearrange("p a h s -> p (a h s)")
        turn, whole, *red = (first[:, c * 2 * B * FR:(c + 1) * 2 * B * FR].rearrange("p (c n) -> p c n", c=2)
                             for c in range(5))
        wqkv_raw = first[:, 10 * B * FR:10 * B * FR + K * QKV].rearrange("p (k m) -> p k m", k=K)
        trig = sb("trig", [P, 2, B, FR])
        cs = sb("cs", [P, 2, B, FR])
        ms1 = sb("ms1", [P, B])
        ln1 = sb("ln1", [P, B])
        rstd1 = sb("rstd1", [P, B])
        xg_hi = sb("xg_hi", [P, 3, K, S], F32R)
        ropeA, ropeB = sb("ropeA", [P, QK]), sb("ropeB", [P, QK])
        qk = sb("qk", [P, 2, NH + 1, HD])
        stack = sb("stack", [P, 2, NH + 1, 3, HD])
        qkT = sb("qkT", [P, 2, NH, S], F32R)
        kT = sb("kT", [P, 2, S], F32R)
        v_sb = sb("v_sb", [P, B, HD])
        top = sb("top", [P, 2, NH], BF16)
        rden = sb("rden", [P, K, S])
        ctxn = sb("ctxn", [P, 2, K, S])
        ctx_hi, ctx_lo = sb("ctx_hi", [P, K, HT], F32R), sb("ctx_lo", [P, K, HT], F32R)
        lnrow = sb("lnrow", [P, HT])
        rstd = sb("rstd", [P, HT])
        sqsum = sb("sqsum", [P, HT])
        h_hi, h_lo = sb("h_hi", [P, K, HT], F32R), sb("h_lo", [P, K, HT], F32R)
        act = sb("act", [P, 2, HT])
        act_hi, act_lo = sb("act_hi", [P, FT, HT], F32R), sb("act_lo", [P, FT, HT], F32R)
        hf = xn_sb[:, 0:NB, :].rearrange("p b h -> p (b h)").rearrange("p (k t) -> p k t", k=K)
        sq = xn_sb[:, NB:B, :].rearrange("p b h -> p (b h)").rearrange("p (k t) -> p k t", k=K)
        hid = [half_e[:, e] for half_e in (
            wgu_raw[:].rearrange("p f g k m -> p (f g k m)").rearrange("p (e t) -> p e t", e=HG),
            first.rearrange("p (e t) -> p e t", e=HG)) for e in range(HG)]
        yln = wd_raw[:].rearrange("p f h -> p (f h)").rearrange("p (k t) -> p k t", k=2 * K)
        x3_hi = qkT[:].rearrange("p a h s -> p (a h s)")[:, 0:K * HT].rearrange("p (k t) -> p k t", k=K)
        x3_lo = qkT[:].rearrange("p a h s -> p (a h s)")[:, K * HT:2 * K * HT].rearrange("p (k t) -> p k t", k=K)

        bank = [ctx.enter_context(nc.psum_tensor(f"bank{i}", [P, 512], F32)) for i in range(8)]
        proj_ps, ctx_ps = bank[0], bank[1]
        score_ps = bank[4:6]

        def pair(b):
            return bank[6:8] if b in (1, 3) else bank[2:4]

        def pair_before(b):
            return {2: 0, 3: 1, 4: 2, 5: 4, 6: 5, 7: 6}.get(b)

        gate_ps, up_ps = bank[6], bank[7]

        ld = {n: sem("ld_" + n) for n in (
            "small", "ident", "pos", "tw1", "tw2", "xT0", "xT1", "xn0", "xn1", "wqkv", "wo", "wgu0", "wgu1",
            "wgu2", "wgu3", "wd", "w1", "w2", "embw", "outw")}
        eps_ready = sem("eps_ready")
        zeroed, consts_ready, negid_ready = sem("zeroed"), sem("consts_ready"), sem("negid_ready")
        wqkv_split, weight_hi, weight_lo = sem("wqkv_split"), sem("weight_hi"), sem("weight_lo")
        scale1_done, gain1_done = sem("scale1_done"), sem("gain1_done")
        scale2_done, gain2_done = sem("scale2_done"), sem("gain2_done")
        scond_done, emb_done, shift_done, lnab_done = (
            sem("scond_done"), sem("emb_done"), sem("shift_done"), sem("lnab_done"))
        table_step, trig_done, ms1_done, ln1_done, rstd1_done, cs_done = (
            sem("table_step"), sem("trig_done"), sem("ms1_done"), sem("ln1_done"), sem("rstd1_done"), sem("cs_done"))
        xg_hi_done, xg_lo_done, proj_done = sem("xg_hi_done"), sem("xg_lo_done"), sem("proj_done")
        rope_mul, rope_done, v_done = sem("rope_mul"), sem("rope_done"), sem("v_done")
        qk_hi_done, qk_lo_done = sem("qk_hi_done"), sem("qk_lo_done")
        turned, kturned, qT_done, kT_done = sem("turned"), sem("kturned"), sem("qT_done"), sem("kT_done")
        s1_done, top_done, st_done, exp_done = sem("s1_done"), sem("top_done"), sem("st_done"), sem("exp_done")
        pv_done, lden_done, rden_done, ctxn_done = (
            sem("pv_done"), sem("lden_done"), sem("rden_done"), sem("ctxn_done"))
        ctx_hi_done, ctx_lo_done = sem("ctx_hi_done"), sem("ctx_lo_done")
        wo_done, x2_done = sem("wo_done"), sem("x2_done")
        sq2_done, sqsum2_done, ms2_done, ln2_done, rstd2_done = (
            sem("sq2_done"), sem("sqsum2_done"), sem("ms2_done"), sem("ln2_done"), sem("rstd2_done"))
        h_done, h_hi_done, h_lo_done = sem("h_done"), sem("h_hi_done"), sem("h_lo_done")
        gate_mm, up_mm, gate_done, act_done = sem("gate_mm"), sem("up_mm"), sem("gate_done"), sem("act_done")
        act_hi_done, act_lo_done = sem("act_hi_done"), sem("act_lo_done")
        down_done, x3_done, x3_hi_done, x3_lo_done = (
            sem("down_done"), sem("x3_done"), sem("x3_hi_done"), sem("x3_lo_done"))
        e1_done, gelu_done, e2_done, y_done = sem("e1_done"), sem("gelu_done"), sem("e2_done"), sem("y_done")
        ysum_done, mean_done, dev_done, sqd_done, sqdsum_done, var_done, lnv_done, rstdv_done = (
            sem("ysum_done"), sem("mean_done"), sem("dev_done"), sem("sqd_done"), sem("sqdsum_done"),
            sem("var_done"), sem("lnv_done"), sem("rstdv_done"))
        z_done, s_done, s_hi_done, s_lo_done = sem("z_done"), sem("s_done"), sem("s_hi_done"), sem("s_lo_done")
        out_mm, fin_done, stored = sem("out_mm"), sem("fin_done"), sem("stored")

        W_WO, W_GU, W_D, W_1, W_OUT = 1, 2, 2 + FT, 2 + 2 * FT, 4 + 2 * FT
        block = ctx.enter_context(nc.Block())

        def half(n):
            return slice(n * HT, (n + 1) * HT)

        def tok(b):
            return slice(b % NB * S, (b % NB + 1) * S)

        @block.sync
        def _(sp):
            sp.dma_start(small_sb[:], small).then_inc(ld["small"], 16)
            sp.dma_start(tw1_sb[:], tw1).then_inc(ld["tw1"], 16)
            sp.dma_start(pos_sb[:], posT).then_inc(ld["pos"], 16)
            sp.dma_start(xn_sb[:, 0:NB], xn[:, 0:NB]).then_inc(ld["xn0"], 16)
            sp.dma_start(res_sb[:, :, half(0)], xT[:, :, half(0)]).then_inc(ld["xT0"], 16)
            sp.dma_start(wqkv_raw, wqkv).then_inc(ld["wqkv"], 16)
            sp.dma_start(id_sb[:], ident).then_inc(ld["ident"], 16)
            sp.dma_start(sq_raw[:], wo).then_inc(ld["wo"], 16)
            sp.dma_start(xn_sb[:, NB:B], xn[:, NB:B]).then_inc(ld["xn1"], 16)
            sp.dma_start(res_sb[:, :, half(1)], xT[:, :, half(1)]).then_inc(ld["xT1"], 16)
            sp.dma_start(tw2_sb[:], tw2).then_inc(ld["tw2"], 16)
            for c in range(4):
                if c == 2:
                    sp.dma_start(wd_raw[:], wd).then_inc(ld["wd"], 16)
                if c >= 2:
                    sp.wait_ge(weight_lo, W_GU + 2 * c - 3)
                r = 2 * c % RAW_TILES
                sp.dma_start(wgu_raw[:, r:r + 2], wgu[:, 2 * c:2 * c + 2]).then_inc(ld[f"wgu{c}"], 16)
            sp.wait_ge(zeroed, 1)
            for r in range(4):
                sp.dma_start(w1_raw[32 * r:32 * r + 32, r::4], w1[:, r::4]).then_inc(ld["w1"], 16)
            sp.dma_start(emb_sb[:], embw).then_inc(ld["embw"], 16)
            sp.dma_start(w2_sb[:], w2).then_inc(ld["w2"], 16)
            sp.dma_start(sq_raw[:], outw).then_inc(ld["outw"], 16)
            for n in range(HALVES):
                for m in range(K):
                    sp.wait_ge(fin_done, K * n + m + 1)
                    sp.dma_start(out[:, m, half(n)], res_sb[:, m, half(n)]).then_inc(stored, 16)
            sp.wait_ge(stored, 16 * HALVES * K)

        @block.gpsimd
        def _(pool):
            nc.gpsimd.memset(avg[:], 1.0 / H).then_inc(consts_ready, 1)
            nc.gpsimd.memset(ones[:], 1.0).then_inc(consts_ready, 1)

            def split(raw, hi, lo, loads):
                for s, n in loads:
                    pool.wait_ge(s, n)
                nc.gpsimd.tensor_copy(hi, raw).then_inc(weight_hi, 1)
                split.n += 1
                pool.wait_ge(weight_hi, split.n)
                nc.gpsimd.tensor_tensor(lo, raw, hi.bitcast(F32), ALU.subtract).then_inc(weight_lo, 1)
            split.n = 0
            split(sq_raw[:], wo_hi[:], wo_lo[:], [(ld["wo"], 16)])
            pool.wait_ge(scale1_done, 1)
            pool.wait_ge(scale2_done, 1)
            nc.gpsimd.memset(w1_raw, 0.0).then_inc(zeroed, 1)
            for f in range(FT):
                split(wgu_raw[:, f % RAW_TILES], wgu_hi[:, f], wgu_lo[:, f], [(ld[f"wgu{f // 2}"], 16)])

            def act_low(n, f):
                pool.wait_ge(act_done, FT * n + f + 1)
                pool.wait_ge(act_hi_done, FT * n + f + 1)
                if n and not f:
                    pool.wait_ge(down_done, K)
                nc.gpsimd.tensor_tensor(act_lo[:, f], act[:, f % 2], act_hi[:, f].bitcast(F32),
                                        ALU.subtract).then_inc(act_lo_done, 1)
            for f in range(FT):
                split(wd_raw[:, f], wd_hi[:, f], wd_lo[:, f], [(ld["wd"], 16)])
                act_low(0, f)
            pool.wait_ge(proj_done, B)
            for c in range(2):
                split(w1_raw[:, 4 * c:4 * c + 4], w1_hi[:, 4 * c:4 * c + 4], w1_lo[:, 4 * c:4 * c + 4], [(ld["w1"], 64)])
            split(sq_raw[:], outw_hi[:], outw_lo[:], [(ld["outw"], 16)])
            for f in range(FT):
                act_low(1, f)

        @block.scalar
        def _(act_e):
            A = nc.scalar.activation

            def mean_square(n):
                act_e.wait_ge(ld[f"xn{n}"], 16)
                if n:
                    act_e.wait_ge(ms1_done, NB * n)
                for b in range(NB * n, NB * n + NB):
                    A(sq_junk(b), xn_sb[:, b], ACT.Square, accum_out=ms1[:, b:b + 1]).then_inc(ms1_done, 1)

            def sq_junk(b):
                return act[:].rearrange("p a t -> p (a t)")[:, b % NB * H:(b % NB + 1) * H]

            def rstd_first(n):
                bs = slice(NB * n, NB * n + NB)
                act_e.wait_ge(ms1_done, NB * n + NB)
                A(ln1[:, bs], ms1[:, bs], ACT.Ln, scale=1.0 / H, bias=eps_rms).then_inc(ln1_done, 1)
                act_e.wait_ge(ln1_done, n + 1)
                A(rstd1[:, bs], ln1[:, bs], ACT.Exp, scale=-0.5).then_inc(rstd1_done, 1)

            eps_rms, eps_ln = eps_sb[:, 0:1], eps_sb[:, 1:2]

            def xg_high(b):
                act_e.wait_ge(ld[f"xT{b // NB}"], 16)
                act_e.wait_ge(gain1_done, K)
                if b >= 3:
                    act_e.wait_ge(proj_done, b - 2)
                for k in range(K):
                    A(xg_hi[:, b % 3, k], res_sb[:, k, b * S:(b + 1) * S], ACT.Copy,
                      scale=gain1[:, k, b:b + 1]).then_inc(xg_hi_done, 1)

            def stack_high(b):
                act_e.wait_ge(rope_done, 2 * (b + 1))
                if b >= 2:
                    act_e.wait_ge(turned, 2 * (b - 1))
                    act_e.wait_ge(kturned, b - 1)
                st = stack[:, b % 2].bitcast(F32R)
                A(st[:, 0:NH, 0], qk[:, b % 2, 0:NH], ACT.Copy).then_inc(qk_hi_done, 1)
                A(st[:, 0:NH, 2], qk[:, b % 2, 0:NH], ACT.Copy).then_inc(qk_hi_done, 1)
                A(st[:, NH, 0:2], qk[:, b % 2, NH:NH + 1].broadcast_to([P, 2, HD]), ACT.Copy).then_inc(qk_hi_done, 1)

            def take_turned(b):
                if b >= 2:
                    act_e.wait_ge(st_done, 2 * (b - 1))
                for g in range(2):
                    act_e.wait_ge(turned, 2 * b + g + 1)
                    A(qkT[0:96, b % 2, HG * g:HG * g + HG].rearrange("p h s -> p (h s)"), pair(b)[g][0:96, :],
                      ACT.Copy).then_inc(qT_done, 1)
                act_e.wait_ge(kturned, b + 1)
                A(kT[0:96, b % 2], score_ps[0][0:96, 0:S], ACT.Copy).then_inc(kT_done, 1)

            def exps(b):
                if b >= 2:
                    act_e.wait_ge(pv_done, b - 1)
                for g in range(2):
                    act_e.wait_ge(st_done, 2 * b + g + 1)
                    A(prob[:, b % 2, HG * g:HG * g + HG].rearrange("p h s -> p (h s)"), pair(b)[g][:, :], ACT.Exp,
                      scale=HD ** -0.5).then_inc(exp_done, 1)

            def reciprocal_of_sum(b):
                act_e.wait_ge(pv_done, b + 1)
                if b >= 1:
                    act_e.wait_ge(ctxn_done, b)
                A(rden[:], ctx_ps[:, K * S:2 * K * S].rearrange("p (k s) -> p k s", k=K), ACT.Ln).then_inc(lden_done, 1)
                act_e.wait_ge(lden_done, b + 1)
                A(rden[:], rden[:], ACT.Exp, scale=-1.0).then_inc(rden_done, 1)

            def ctx_high(b):
                act_e.wait_ge(ctxn_done, b + 1)
                if b == NB:
                    act_e.wait_ge(wo_done, K)
                A(ctx_hi[:, :, tok(b)], ctxn[:, b % 2], ACT.Copy).then_inc(ctx_hi_done, 1)

            def rms_second(n):
                for k in range(K):
                    act_e.wait_ge(x2_done, K * n + k + 1)
                    if n:
                        act_e.wait_ge(sqsum2_done, n)
                    A(sq[:, k], res_sb[:, k, half(n)], ACT.Square).then_inc(sq2_done, 1)
                act_e.wait_ge(ms2_done, n + 1)
                if n:
                    act_e.wait_ge(h_done, NB * K * n)
                A(lnrow[:], bank[6 if n == 0 else 4][:, :], ACT.Ln, bias=eps_rms).then_inc(ln2_done, 1)
                act_e.wait_ge(ln2_done, n + 1)
                A(rstd[:], lnrow[:], ACT.Exp, scale=-0.5).then_inc(rstd2_done, 1)

            def h_high(n):
                act_e.wait_ge(h_done, NB * K * (n + 1))
                if n:
                    act_e.wait_ge(up_mm, FT * n)
                A(h_hi[:], hf, ACT.Copy).then_inc(h_hi_done, 1)

            def silu(n, f):
                i = FT * n + f
                act_e.wait_ge(gate_mm, i + 1)
                if i >= 2:
                    act_e.wait_ge(act_hi_done, i - 1)
                    act_e.wait_ge(act_lo_done, i - 1)
                A(act[:, i % 2], gate_ps[:, :], ACT.Silu).then_inc(gate_done, 1)

            def act_high(n, f):
                i = FT * n + f
                act_e.wait_ge(act_done, i + 1)
                if n and not f:
                    act_e.wait_ge(down_done, K)
                A(act_hi[:, f], act[:, i % 2], ACT.Copy).then_inc(act_hi_done, 1)

            def x3_high(n):
                for m in range(K):
                    act_e.wait_ge(x3_done, K * n + m + 1)
                    if n and not m:
                        act_e.wait_ge(e1_done, E * n)
                    A(x3_hi[:, m], res_sb[:, m, half(n)], ACT.Copy).then_inc(x3_hi_done, 1)

            def gelu(n, e):
                act_e.wait_ge(e1_done, E * n + e + 1)
                if n and e % 4 == 0:
                    act_e.wait_ge(e2_done, 2 * n - 1 + e // 4)
                A(hid[e], bank[(0, 1, 6, 7)[e % 4]][:, :], ACT.Gelu,
                  bias=small_sb[:, C_B1 + e:C_B1 + e + 1]).then_inc(gelu_done, 1)

            def norm_squares(n):
                for k in range(K):
                    act_e.wait_ge(dev_done, K * n + k + 1)
                    if n:
                        act_e.wait_ge(sqdsum_done, n)
                    A(sq[:, k], yln[:, 2 + k], ACT.Square).then_inc(sqd_done, 1)

            def norm_rstd(n):
                act_e.wait_ge(var_done, n + 1)
                if n:
                    act_e.wait_ge(z_done, K * n)
                A(lnrow[:], bank[5][:, :], ACT.Ln, bias=eps_ln).then_inc(lnv_done, 1)
                act_e.wait_ge(lnv_done, n + 1)
                A(rstd[:], lnrow[:], ACT.Exp, scale=-0.5).then_inc(rstdv_done, 1)

            def norm_silu(n):
                act_e.wait_ge(lnab_done, 3)
                for k in range(K):
                    act_e.wait_ge(z_done, K * n + k + 1)
                    for j in range(NB):
                        b = NB * n + j
                        A(hf[:, k, j * S:(j + 1) * S], yln[:, k, j * S:(j + 1) * S], ACT.Silu,
                          scale=lnA[:, k, b:b + 1], bias=lnB[:, k, b:b + 1]).then_inc(s_done, 1)

            def s_high(n):
                act_e.wait_ge(s_done, NB * K * (n + 1))
                if n:
                    act_e.wait_ge(out_mm, K * n)
                A(h_hi[:], hf, ACT.Copy).then_inc(s_hi_done, 1)

            mean_square(0)
            act_e.wait_ge(table_step, TABLE_READY)
            A(trig[:].rearrange("p c b f -> p (c b f)"), red[2].rearrange("p c n -> p (c n)"),
              ACT.Sin).then_inc(trig_done, 1)
            nc.scalar.preload_act_table_set("natural_log_exp_and_others")
            act_e.wait_ge(eps_ready, 2)
            act_e.wait_ge(ld["small"], 16)
            rstd_first(0)
            xg_high(0)
            xg_high(1)
            stack_high(0)
            take_turned(0)
            xg_high(2)
            for b in range(NB):
                stack_high(b + 1)
                if b == 0:
                    mean_square(1)
                    rstd_first(1)
                take_turned(b + 1)
                exps(b)
                xg_high(b + 3)
                reciprocal_of_sum(b)
                ctx_high(b)
            rms_second(0)
            exps(4)
            stack_high(5)
            xg_high(7)
            take_turned(5)
            reciprocal_of_sum(4)
            ctx_high(4)
            h_high(0)
            act_e.wait_ge(ld["small"], 16)
            A(scond[:].rearrange("p k b -> p (k b)"), small_sb[:, C_COND:C_COND + K * B], ACT.Silu).then_inc(scond_done, 1)
            f = 0
            for b in range(5, B):
                if f:
                    nc.scalar.preload_act_table_set("natural_log_exp_and_others")
                exps(b)
                if b + 1 < B:
                    stack_high(b + 1)
                    take_turned(b + 1)
                reciprocal_of_sum(b)
                ctx_high(b)
                for _ in range(2):
                    silu(0, f)
                    act_high(0, f)
                    f += 1
            while f < FT:
                silu(0, f)
                act_high(0, f)
                f += 1
            nc.scalar.preload_act_table_set("natural_log_exp_and_others")
            rms_second(1)
            h_high(1)
            x3_high(0)
            for f in range(FT):
                silu(1, f)
                act_high(1, f)
            for e in range(E):
                gelu(0, e)
            norm_squares(0)
            x3_high(1)
            nc.scalar.preload_act_table_set("natural_log_exp_and_others")
            norm_rstd(0)
            for e in range(E):
                gelu(1, e)
            norm_silu(0)
            s_high(0)
            norm_squares(1)
            nc.scalar.preload_act_table_set("natural_log_exp_and_others")
            norm_rstd(1)
            norm_silu(1)
            s_high(1)

        @block.vector
        def _(dve):
            TT, TS, STT = nc.vector.tensor_tensor, nc.vector.tensor_scalar, nc.vector.scalar_tensor_tensor

            def col(c, n=1):
                return small_sb[:, c:c + n]

            nc.vector.memset(eps_sb[:, 0:1], RMS_EPS).then_inc(eps_ready, 1)
            nc.vector.memset(eps_sb[:, 1:2], LN_EPS).then_inc(eps_ready, 1)

            def rotary_tables():
                dve.wait_ge(ld["pos"], 16)
                dve.wait_ge(ld["small"], 16)
                n = [0]

                def then(ins):
                    n[0] += 1
                    ins.then_inc(table_step, 1)
                    dve.wait_ge(table_step, n[0])
                both = [P, 2, B * FR]
                then(nc.vector.tensor_copy(posf[:], pos_sb[:]))
                then(TT(ang[:].rearrange("p (b f) -> p b f", b=B),
                        posf[:].rearrange("p (b f) -> p b f", f=1).broadcast_to([P, B, FR]),
                        col(C_INVF, FR).rearrange("p (b f) -> p b f", b=1).broadcast_to([P, B, FR]), ALU.mult))
                then(TS(turn[:, 0], ang[:], 0.5 / PI, 0.25, ALU.mult, ALU.add))
                then(TS(turn[:, 1], ang[:], 0.5 / PI, None, ALU.mult))
                then(TS(whole, turn, MAGIC, -MAGIC, ALU.add, ALU.add))
                then(STT(red[0], whole, -TAU_A, ang[:].rearrange("p (c n) -> p c n", c=1).broadcast_to(both),
                         ALU.mult, ALU.add))
                then(STT(red[1], whole, -TAU_B, red[0], ALU.mult, ALU.add))
                then(STT(red[0], whole, -TAU_C, red[1], ALU.mult, ALU.add))
                then(TS(red[0][:, 0], red[0][:, 0], PI / 2, None, ALU.add))
                TS(red[2], red[0], 3.1415925, -3.1415925, ALU.min, ALU.max).then_inc(table_step, 1)
                assert n[0] + 1 == TABLE_READY

            def scaled_table(n):
                dve.wait_ge(trig_done, 1)
                dve.wait_ge(rstd1_done, n + 1)
                for c in range(2):
                    bs = slice(NB * n, NB * n + NB)
                    TT(cs[:, c, bs], trig[:, c, bs],
                       rstd1[:, bs].rearrange("p (b f) -> p b f", f=1).broadcast_to([P, NB, FR]),
                       ALU.mult).then_inc(cs_done, 1)

            def gains(ps, w_col, gain, mm_done, done):
                dve.wait_ge(mm_done, 1)
                for m in range(K):
                    TS(gain[:, m], ps[:, m * B:(m + 1) * B], 1.0, col(w_col + m), ALU.add, ALU.mult).then_inc(done, 1)

            def xg_low(b):
                for k in range(K):
                    dve.wait_ge(xg_hi_done, K * b + k + 1)
                    if b >= 3 and k == 0:
                        dve.wait_ge(proj_done, b - 2)
                    STT(xg_lo[:, b % 3, k], res_sb[:, k, b * S:(b + 1) * S], gain1[:, k, b:b + 1],
                        xg_hi[:, b % 3, k].bitcast(F32), ALU.mult, ALU.subtract).then_inc(xg_lo_done, 1)

            def rope(b):
                dve.wait_ge(proj_done, b + 1)
                dve.wait_ge(cs_done, 2 * (b // NB + 1))
                if b >= 1:
                    dve.wait_ge(rope_done, 2 * b)
                heads = [P, 2 * (NH + 1), FR]
                for c, o in ((0, ropeA), (1, ropeB)):
                    TT(o[:].rearrange("p (h f) -> p h f", f=FR), proj_ps[:, 0:QK].rearrange("p (h f) -> p h f", f=FR),
                       cs[:, c, b:b + 1].broadcast_to(heads), ALU.mult).then_inc(rope_mul, 1)
                TS(v_sb[:, b], proj_ps[:, QK:QKV], rstd1[:, b:b + 1], None, ALU.mult).then_inc(v_done, 1)
                a = ropeA[:].rearrange("p (h c f) -> p h c f", c=2, f=FR)
                s = ropeB[:].rearrange("p (h c f) -> p h c f", c=2, f=FR)
                dve.wait_ge(rope_mul, 2 * (b + 1))
                if b >= 2:
                    dve.wait_ge(qk_hi_done, 3 * (b - 1))
                    dve.wait_ge(qk_lo_done, 2 * (b - 1))
                TT(qk[:, b % 2, :, 0:FR], a[:, :, 0], s[:, :, 1], ALU.subtract).then_inc(rope_done, 1)
                TT(qk[:, b % 2, :, FR:HD], a[:, :, 1], s[:, :, 0], ALU.add).then_inc(rope_done, 1)

            def stack_low(b):
                dve.wait_ge(rope_done, 2 * (b + 1))
                dve.wait_ge(qk_hi_done, 3 * (b + 1))
                if b >= 2:
                    dve.wait_ge(turned, 2 * (b - 1))
                    dve.wait_ge(kturned, b - 1)
                st = stack[:, b % 2]
                TT(st[:, 0:NH, 1].bitcast(F32R), qk[:, b % 2, 0:NH], st[:, 0:NH, 0], ALU.subtract).then_inc(qk_lo_done, 1)
                TT(st[:, NH, 2].bitcast(F32R), qk[:, b % 2, NH], st[:, NH, 0], ALU.subtract).then_inc(qk_lo_done, 1)

            def maxima(b):
                if b >= 2:
                    dve.wait_ge(st_done, 2 * (b - 1))
                dve.wait_ge(s1_done, 2 * (b + 1))
                for g in range(2):
                    nc.vector.tensor_reduce(top[:, b % 2, HG * g:HG * g + HG],
                                            score_ps[g][:, :].rearrange("p (h t) -> p h t", h=HG),
                                            AX.X, ALU.max).then_inc(top_done, 1)

            def context(b):
                dve.wait_ge(rden_done, b + 1)
                if b >= 2:
                    dve.wait_ge(ctx_hi_done, b - 1)
                    dve.wait_ge(ctx_lo_done, b - 1)
                TT(ctxn[:, b % 2], ctx_ps[:, 0:K * S].rearrange("p (k s) -> p k s", k=K), rden[:],
                   ALU.mult).then_inc(ctxn_done, 1)

            def context_low(b):
                dve.wait_ge(ctx_hi_done, b + 1)
                if b == NB:
                    dve.wait_ge(wo_done, K)
                TT(ctx_lo[:, :, tok(b)], ctxn[:, b % 2], ctx_hi[:, :, tok(b)].bitcast(F32),
                   ALU.subtract).then_inc(ctx_lo_done, 1)

            def x2(n):
                for m in range(K):
                    dve.wait_ge(wo_done, K * n + m + 1)
                    r = res_sb[:, m, half(n)]
                    TT(r, bank[(6 if n == 0 else 4) + m][:, :], r, ALU.add).then_inc(x2_done, 1)

            def square_sum(n):
                dve.wait_ge(sq2_done, K * (n + 1))
                TT(sqsum[:], sq[:, 0], sq[:, 1], ALU.add).then_inc(sqsum2_done, 1)

            def normed(n):
                dve.wait_ge(rstd2_done, n + 1)
                dve.wait_ge(gain2_done, K)
                for k in range(K):
                    for j in range(NB):
                        b = NB * n + j
                        STT(hf[:, k, j * S:(j + 1) * S], res_sb[:, k, b * S:(b + 1) * S], gain2[:, k, b:b + 1],
                            rstd[:, j * S:(j + 1) * S], ALU.mult, ALU.mult).then_inc(h_done, 1)

            def normed_low(n):
                dve.wait_ge(h_hi_done, n + 1)
                if n:
                    dve.wait_ge(up_mm, FT * n)
                TT(h_lo[:], hf, h_hi[:].bitcast(F32), ALU.subtract).then_inc(h_lo_done, 1)

            def gated(n, f):
                i = FT * n + f
                dve.wait_ge(gate_done, i + 1)
                dve.wait_ge(up_mm, i + 1)
                TT(act[:, i % 2], up_ps[:, :], act[:, i % 2], ALU.mult).then_inc(act_done, 1)

            def x3(n):
                for m in range(K):
                    dve.wait_ge(down_done, K * n + m + 1)
                    r = res_sb[:, m, half(n)]
                    TT(r, bank[2 + m][:, :], r, ALU.add).then_inc(x3_done, 1)

            def x3_low(n):
                for m in range(K):
                    dve.wait_ge(x3_hi_done, K * n + m + 1)
                    if n and not m:
                        dve.wait_ge(e1_done, E * n)
                    TT(x3_lo[:, m], res_sb[:, m, half(n)], x3_hi[:, m].bitcast(F32), ALU.subtract).then_inc(x3_lo_done, 1)

            def expert_out(n, g):
                dve.wait_ge(e2_done, 2 * n + g + 1)
                if n and not g:
                    dve.wait_ge(z_done, K * n)
                    dve.wait_ge(s_done, NB * K * n)
                TS(yln[:, g], bank[(4, 5)[g]][:, :], col(C_B2 + g), None, ALU.add).then_inc(y_done, 1)

            def centred(n):
                dve.wait_ge(mean_done, n + 1)
                if n:
                    dve.wait_ge(z_done, K * n)
                for k in range(K):
                    TT(yln[:, 2 + k], yln[:, k], bank[4][:, :], ALU.subtract).then_inc(dev_done, 1)

            def y_sum(n):
                dve.wait_ge(y_done, 2 * (n + 1))
                if n:
                    dve.wait_ge(var_done, n)
                TT(sqsum[:], yln[:, 0], yln[:, 1], ALU.add).then_inc(ysum_done, 1)

            def dev_sum(n):
                dve.wait_ge(sqd_done, K * (n + 1))
                dve.wait_ge(mean_done, n + 1)
                TT(sqsum[:], sq[:, 0], sq[:, 1], ALU.add).then_inc(sqdsum_done, 1)

            def standard(n):
                dve.wait_ge(rstdv_done, n + 1)
                for k in range(K):
                    TT(yln[:, k], yln[:, 2 + k], rstd[:], ALU.mult).then_inc(z_done, 1)

            def s_low(n):
                dve.wait_ge(s_hi_done, n + 1)
                if n:
                    dve.wait_ge(out_mm, K * n)
                TT(h_lo[:], hf, h_hi[:].bitcast(F32), ALU.subtract).then_inc(s_lo_done, 1)

            def finish(n):
                for m in range(K):
                    dve.wait_ge(out_mm, K * n + m + 1)
                    r = res_sb[:, m, half(n)]
                    STT(r, bank[2 + m][:, :], col(C_OUTB + m), r, ALU.add, ALU.add).then_inc(fin_done, 1)

            def layer_norm_affine():
                dve.wait_ge(emb_done, 1)
                for m in range(2 * K):
                    TS(shiftb[:, m], bank[7][:, m * B:(m + 1) * B], col(C_EMBB + m), None, ALU.add).then_inc(shift_done, 1)
                dve.wait_ge(shift_done, 2 * K)
                for m in range(K):
                    TS(lnA[:, m], shiftb[:, m], 1.0, col(C_LNG + m), ALU.add, ALU.mult).then_inc(shift_done, 1)
                    TS(lnB[:, m], shiftb[:, m], 1.0, col(C_LNB + m), ALU.add, ALU.mult).then_inc(shift_done, 1)
                dve.wait_ge(shift_done, 4 * K)
                TT(lnB[:], lnB[:], shiftb[:, K:2 * K], ALU.add).then_inc(lnab_done, 3)

            rotary_tables()
            gains(bank[7], C_LN1W, gain1, scale1_done, gain1_done)
            dve.wait_ge(ld["wqkv"], 16)
            nc.vector.tensor_copy(wqkv_hi, wqkv_raw).then_inc(wqkv_split, 1)
            dve.wait_ge(wqkv_split, 1)
            TT(wqkv_lo, wqkv_raw, wqkv_hi.bitcast(F32), ALU.subtract).then_inc(wqkv_split, 1)
            dve.wait_ge(gain1_done, K)
            xg_low(0)
            dve.wait_ge(ld["ident"], 16)
            TS(negid[:], id_sb[:], -1.0, None, ALU.mult).then_inc(negid_ready, 1)
            scaled_table(0)
            rope(0)
            stack_low(0)
            xg_low(1)
            gains(bank[6], C_LN2W, gain2, scale2_done, gain2_done)
            for b in range(NB):
                rope(b + 1)
                stack_low(b + 1)
                if b == 0:
                    scaled_table(1)
                maxima(b)
                xg_low(b + 2)
                context(b)
                context_low(b)
            x2(0)
            square_sum(0)
            maxima(4)
            rope(5)
            stack_low(5)
            xg_low(6)
            context(4)
            context_low(4)
            normed(0)
            normed_low(0)
            maxima(5)
            xg_low(7)
            f = 0
            for b in range(5, B):
                if b + 1 < B:
                    rope(b + 1)
                    stack_low(b + 1)
                context(b)
                context_low(b)
                gated(0, f)
                f += 1
                if b + 1 < B:
                    maxima(b + 1)
                gated(0, f)
                f += 1
            while f < FT:
                gated(0, f)
                f += 1
            x2(1)
            square_sum(1)
            normed(1)
            normed_low(1)
            x3(0)
            x3_low(0)
            for f in range(FT):
                gated(1, f)
            layer_norm_affine()
            expert_out(0, 0)
            expert_out(0, 1)
            y_sum(0)
            centred(0)
            dev_sum(0)
            x3(1)
            x3_low(1)
            standard(0)
            expert_out(1, 0)
            expert_out(1, 1)
            y_sum(1)
            s_low(0)
            centred(1)
            dev_sum(1)
            finish(0)
            standard(1)
            s_low(1)
            finish(1)

        @block.tensor
        def _(pe):
            MM = nc.tensor.matmul

            def mm3(out_ap, parts, first=True, last=True):
                for i, (lh, ll, rh, rl) in enumerate(parts):
                    MM(out_ap, lh, rh, start=first and i == 0, stop=False)
                    MM(out_ap, lh, rl, start=False, stop=False)
                    mm = MM(out_ap, ll, rh, start=False, stop=last and i == len(parts) - 1)
                return mm

            def scale_of(tw_sb, ps, load, done):
                pe.wait_ge(ld["small"], 16)
                pe.wait_ge(load, 16)
                for m in range(K):
                    for k in range(K):
                        mm = MM(ps[:, m * B:(m + 1) * B], tw_sb[:, k, m * P:(m + 1) * P],
                                small_sb[:, C_COND + k * B:C_COND + (k + 1) * B], start=k == 0, stop=k == K - 1)
                mm.then_inc(done, 1)

            def project(b):
                if b == 0:
                    pe.wait_ge(wqkv_split, 2)
                else:
                    pe.wait_ge(rope_mul, 2 * b)
                    pe.wait_ge(v_done, b)
                pe.wait_ge(xg_hi_done, K * (b + 1))
                pe.wait_ge(xg_lo_done, K * (b + 1))
                mm3(proj_ps[:, 0:QKV], [(xg_hi[:, b % 3, k], xg_lo[:, b % 3, k], wqkv_hi[:, k], wqkv_lo[:, k])
                                        for k in range(K)]).then_inc(proj_done, 1)

            def turn_queries(b):
                pe.wait_ge(qk_hi_done, 3 * (b + 1))
                pe.wait_ge(qk_lo_done, 2 * (b + 1))
                if b == 0:
                    pe.wait_ge(ld["ident"], 16)
                if b == 1:
                    pe.wait_ge(gain1_done, K)
                    pe.wait_ge(gain2_done, K)
                if pair_before(b) is not None:
                    pe.wait_ge(exp_done, 2 * (pair_before(b) + 1))
                for g in range(2):
                    for h in range(HG):
                        mm = nc.tensor.transpose(pair(b)[g][0:96, h * S:(h + 1) * S],
                                                 stack[:, b % 2, HG * g + h].rearrange("p c d -> p (c d)"), id_sb[:])
                    mm.then_inc(turned, 1)

            def turn_key(b):
                if b >= 1:
                    pe.wait_ge(top_done, 2 * b)
                nc.tensor.transpose(score_ps[0][0:96, 0:S], stack[:, b % 2, NH].rearrange("p c d -> p (c d)"),
                                    id_sb[:]).then_inc(kturned, 1)

            def scores_for_max(b):
                pe.wait_ge(kT_done, b + 1)
                for g in range(2):
                    pe.wait_ge(qT_done, 2 * b + g + 1)
                    for h in range(HG):
                        mm = MM(score_ps[g][:, h * S:(h + 1) * S], qkT[0:96, b % 2, HG * g + h], kT[0:96, b % 2],
                                start=True, stop=True)
                    mm.then_inc(s1_done, 1)

            def scores_transposed(b):
                if b == 0:
                    pe.wait_ge(negid_ready, 1)
                for g in range(2):
                    ps = pair(b)[g]
                    MM(ps[:, :], kT[0:96, b % 2], qkT[0:96, b % 2, HG * g:HG * g + HG].rearrange("p h s -> p (h s)"),
                       start=True, stop=False)
                    pe.wait_ge(top_done, 2 * b + g + 1)
                    for h in range(HG):
                        mm = MM(ps[:, h * S:(h + 1) * S],
                                top[:, b % 2, HG * g + h:HG * g + h + 1].broadcast_to([P, S]), negid[:],
                                start=False, stop=h == HG - 1)
                    mm.then_inc(st_done, 1)

            def weigh_values(b):
                pe.wait_ge(exp_done, 2 * (b + 1))
                pe.wait_ge(v_done, b + 1)
                if b == 0:
                    pe.wait_ge(consts_ready, 2)
                if b >= 1:
                    pe.wait_ge(ctxn_done, b)
                for c, w in ((0, v_sb[:, b]), (1, ones[:])):
                    for r in range(4):
                        mm = MM(ctx_ps[32 * r:32 * r + 32, c * K * S:(c + 1) * K * S], w,
                                prob[:, b % 2, r::4], start=True, stop=True)
                mm.then_inc(pv_done, 1)

            def attn_out(n):
                pe.wait_ge(weight_lo, W_WO)
                pe.wait_ge(ctx_hi_done, NB * (n + 1))
                pe.wait_ge(ctx_lo_done, NB * (n + 1))
                if n == 0:
                    pe.wait_ge(exp_done, 2 * NB)
                for m in range(K):
                    ms = slice(m * P, (m + 1) * P)
                    mm3(bank[(6 if n == 0 else 4) + m][:, :],
                        [(wo_hi[:, k, ms], wo_lo[:, k, ms], ctx_hi[:, k], ctx_lo[:, k])
                         for k in range(K)]).then_inc(wo_done, 1)

            def mean_of_squares(n):
                pe.wait_ge(sqsum2_done, n + 1)
                pe.wait_ge(x2_done, K * n + 1)
                MM(bank[6 if n == 0 else 4][:, :], avg[:], sqsum[:], start=True, stop=True).then_inc(ms2_done, 1)

            def gate_or_up(n, f, u):
                i = FT * n + f
                if f == 0:
                    pe.wait_ge(h_hi_done, n + 1)
                    pe.wait_ge(h_lo_done, n + 1)
                pe.wait_ge(weight_lo, W_GU + f)
                if u == 0:
                    if i:
                        pe.wait_ge(gate_done, i)
                    else:
                        pe.wait_ge(ln2_done, 1)
                else:
                    if i:
                        pe.wait_ge(act_done, i)
                    else:
                        pe.wait_ge(x2_done, K)
                mm3((gate_ps, up_ps)[u][:, :], [(wgu_hi[:, f, u, k], wgu_lo[:, f, u, k], h_hi[:, k], h_lo[:, k])
                                                for k in range(K)]).then_inc((gate_mm, up_mm)[u], 1)

            def down(n, m):
                if m == 0:
                    pe.wait_ge(act_hi_done, FT * (n + 1))
                    pe.wait_ge(act_lo_done, FT * (n + 1))
                    pe.wait_ge(weight_lo, W_D + FT - 1)
                    if n == 0:
                        pe.wait_ge(exp_done, 2 * B)
                if n:
                    pe.wait_ge(x3_done, K)
                ms = slice(m * P, (m + 1) * P)
                mm3(bank[2 + m][:, :], [(wd_hi[:, f, ms], wd_lo[:, f, ms], act_hi[:, f], act_lo[:, f])
                                        for f in range(FT)]).then_inc(down_done, 1)

            def expert_in(n, e):
                k = e // 4
                pe.wait_ge(x3_hi_done, K * n + k + 1)
                pe.wait_ge(x3_lo_done, K * n + k + 1)
                pe.wait_ge(weight_lo, W_1 + k)
                if e >= 4 or n:
                    pe.wait_ge(gelu_done, E * n + e - 3)
                elif e < 2:
                    pe.wait_ge(ctxn_done, B)
                else:
                    pe.wait_ge(act_done, 2 * FT)
                mm3(bank[(0, 1, 6, 7)[e % 4]][:, :],
                    [(w1_hi[:, e], w1_lo[:, e], x3_hi[:, k], x3_lo[:, k])]).then_inc(e1_done, 1)

            def expert_out(n, g):
                pe.wait_ge(gelu_done, E * n + 4 * g + 4)
                pe.wait_ge(ld["w2"], 16)
                if n == 0:
                    pe.wait_ge(x2_done, 2 * K)
                    pe.wait_ge(ln2_done, 2)
                elif g == 0:
                    pe.wait_ge(dev_done, K)
                else:
                    pe.wait_ge(lnv_done, 1)
                for r in range(4):
                    mm = MM(bank[(4, 5)[g]][32 * r:32 * r + 32, :], w2_sb[:, 4 * g + r], hid[4 * g + r],
                            start=True, stop=True)
                mm.then_inc(e2_done, 1)

            def mean(n):
                pe.wait_ge(ysum_done, n + 1)
                MM(bank[4][:, :], avg[:], sqsum[:], start=True, stop=True).then_inc(mean_done, 1)

            def variance(n):
                pe.wait_ge(sqdsum_done, n + 1)
                MM(bank[5][:, :], avg[:], sqsum[:], start=True, stop=True).then_inc(var_done, 1)

            def last_product(n):
                pe.wait_ge(s_hi_done, n + 1)
                pe.wait_ge(s_lo_done, n + 1)
                pe.wait_ge(weight_lo, W_OUT)
                pe.wait_ge(x3_done, 2 * K)
                if n:
                    pe.wait_ge(fin_done, K)
                for m in range(K):
                    ms = slice(m * P, (m + 1) * P)
                    mm3(bank[2 + m][:, :], [(outw_hi[:, k, ms], outw_lo[:, k, ms], h_hi[:, k], h_lo[:, k])
                                            for k in range(K)]).then_inc(out_mm, 1)

            def embedding():
                pe.wait_ge(scond_done, 1)
                pe.wait_ge(ld["embw"], 16)
                pe.wait_ge(act_done, 2 * FT)
                for m in range(2 * K):
                    for k in range(K):
                        mm = MM(bank[7][:, m * B:(m + 1) * B], emb_sb[:, k, m * P:(m + 1) * P], scond[:, k],
                                start=k == 0, stop=k == K - 1)
                mm.then_inc(emb_done, 1)

            scale_of(tw1_sb, bank[7], ld["tw1"], scale1_done)
            project(0)
            scale_of(tw2_sb, bank[6], ld["tw2"], scale2_done)
            turn_queries(0)
            turn_key(0)
            project(1)
            scores_for_max(0)
            for b in range(NB):
                project(b + 2)
                turn_queries(b + 1)
                turn_key(b + 1)
                scores_transposed(b)
                scores_for_max(b + 1)
                weigh_values(b)
            attn_out(0)
            scores_transposed(4)
            mean_of_squares(0)
            project(6)
            weigh_values(4)
            turn_queries(5)
            turn_key(5)
            scores_for_max(5)
            f = 0
            for b in range(5, B):
                scores_transposed(b)
                gate_or_up(0, f, 0)
                if b + 2 < B:
                    project(b + 2)
                weigh_values(b)
                gate_or_up(0, f, 1)
                f += 1
                if b + 1 < B:
                    turn_queries(b + 1)
                    turn_key(b + 1)
                gate_or_up(0, f, 0)
                if b + 1 < B:
                    scores_for_max(b + 1)
                gate_or_up(0, f, 1)
                f += 1
            while f < FT:
                gate_or_up(0, f, 0)
                gate_or_up(0, f, 1)
                f += 1
            attn_out(1)
            down(0, 0)
            mean_of_squares(1)
            down(0, 1)
            for f in range(FT):
                gate_or_up(1, f, 0)
                gate_or_up(1, f, 1)
            embedding()
            pe.wait_ge(shift_done, 2 * K)
            for g in range(2):
                for e in range(4 * g, 4 * g + 4):
                    expert_in(0, e)
                expert_out(0, g)
            down(1, 0)
            mean(0)
            down(1, 1)
            variance(0)
            for g in range(2):
                for e in range(4 * g, 4 * g + 4):
                    expert_in(1, e)
                expert_out(1, g)
            last_product(0)
            mean(1)
            variance(1)
            last_product(1)


def kernel(x, pos_BxS, cond_2048, L0_cond_ln1_w, L0_cond_ln1_tw, L0_cond_ln2_w, L0_cond_ln2_tw, L0_cond_Wq,
           L0_cond_Wk, L0_cond_Wv, L0_cond_Wo, L0_cond_Wg, L0_cond_Wu, L0_cond_Wd, L1_cond_W1, L1_cond_b1,
           L1_cond_W2, L1_cond_b2, L1_cond_emb_W, L1_cond_emb_b, L1_cond_ln_g, L1_cond_ln_b, L1_cond_out_W,
           L1_cond_out_b):
    import numpy as np
    import concourse.bacc as bacc
    from concourse.bass_utils import run_bass_kernel_spmd

    def tiles(a, axis=0):
        a = np.asarray(a)
        return a.reshape(a.shape[0] // P, P, -1).transpose(1, 0, 2)

    def turned(w):
        return tiles(np.asarray(w).T)

    x = np.asarray(x)
    inv_freq = (np.float32(1.0) / np.float32(10000.0) ** (np.arange(0, HD, 2, dtype=np.float32) / np.float32(HD)))
    small = np.concatenate(
        [np.asarray(a).reshape(-1, P).T for a in (L0_cond_ln1_w, L0_cond_ln2_w, L1_cond_ln_g, L1_cond_ln_b,
                                                  L1_cond_out_b, L1_cond_b2, L1_cond_emb_b, L1_cond_b1)]
        + [tiles(np.asarray(cond_2048).T).reshape(P, K * B), np.tile(inv_freq.astype(np.float32), (P, 1))], axis=1)
    wg, wu = (np.asarray(w).reshape(FT, P, K, P) for w in (L0_cond_Wg, L0_cond_Wu))
    arrays = {
        "xT": tiles(x.reshape(T, H).T),
        "xn": x.transpose(1, 0, 2),
        "small": small,
        "posT": np.asarray(pos_BxS).T,
        "ident": np.eye(P, dtype=np.float32),
        "tw1": turned(L0_cond_ln1_tw),
        "tw2": turned(L0_cond_ln2_tw),
        "wqkv": turned(np.concatenate([np.asarray(w) for w in (L0_cond_Wq, L0_cond_Wk, L0_cond_Wv)])),
        "wo": turned(L0_cond_Wo),
        "wgu": np.stack([wg, wu], axis=1).transpose(4, 0, 1, 3, 2),
        "wd": turned(L0_cond_Wd),
        "w1": np.asarray(L1_cond_W1).transpose(1, 0, 2),
        "w2": np.asarray(L1_cond_W2).transpose(1, 0, 2),
        "embw": tiles(L1_cond_emb_W),
        "outw": tiles(L1_cond_out_W),
    }
    nc = bacc.Bacc("TRN2", target_bir_lowering=False, num_devices=1)
    feed, args = {}, []
    for name, a in arrays.items():
        a = np.ascontiguousarray(a)
        feed[f"in_{name}"] = a
        args.append(nc.dram_tensor(f"in_{name}", a.shape, mybir.dt.from_np(a.dtype), kind="ExternalInput").ap())
    args.append(nc.dram_tensor("out_yT", (P, K, T), F32, kind="ExternalOutput").ap())
    cond_block_kernel(nc, *args)
    r = run_bass_kernel_spmd(nc, [feed], core_ids=[0])
    yT = r.results[0]["out_yT"]
    return yT.transpose(1, 0, 2).reshape(H, T).T.reshape(B, S, H)
```

```python
from contextlib import ExitStack

import concourse.bass as bass
from concourse import mybir

F32 = mybir.dt.float32
F32R = mybir.dt.float32r
BF16 = mybir.dt.bfloat16
I32 = mybir.dt.int32
ALU = mybir.AluOpType
ACT = mybir.ActivationFunctionType
AX = mybir.AxisListType

P = 128
B, S, H = 8, 128, 256
T = B * S
K = H // P
NH, HD = 8, 32
QK = (NH + 1) * HD
QKV = QK + HD
FR = HD // 2
INTER = 1024
FT = INTER // P
E, LAT, FFN = 8, 32, 128
NB = 4
HT = NB * S
HALVES = B // NB
QT = HT // 2
QS = QT // S
QUARTERS = T // QT
HG = 4
RMS_EPS, LN_EPS = 1e-6, 1e-5
PI = 3.14159265358979
MAGIC = 1.5 * 2.0 ** 23
TAU_A = 6.28125
TAU_B = 1.934051513671875e-3
TAU_C = 2 * PI - TAU_A - TAU_B

RAW_TILES = 4
TABLE_READY = 10

C_LN1W, C_LN2W, C_LNG, C_LNB, C_OUTB, C_B2, C_EMBB, C_B1, C_COND, C_INVF, C_END = (
    0, 2, 4, 6, 8, 10, 12, 16, 24, 40, 56)


def cond_block_kernel(nc, xT, xn, small, posT, ident, tw1, tw2, wqkv, wo, wgu, wd, w1, w2, embw, outw, out):
    ctx = ExitStack()
    with ctx:
        def sb(name, shape, dt=F32):
            return ctx.enter_context(nc.sbuf_tensor(name, shape, dt))

        def sem(name):
            return ctx.enter_context(nc.semaphore(name))

        res_sb = sb("res_sb", [P, K, T])
        xn_sb = sb("xn_sb", [P, B, H])
        small_sb = sb("small_sb", [P, C_END])
        pos_sb = sb("pos_sb", [P, B], I32)
        id_sb = sb("id_sb", [P, P])
        tw_sb = sb("tw_sb", [P, 2, K, H])
        tw1_sb, tw2_sb = tw_sb[:, 0], tw_sb[:, 1]
        emb_sb = sb("emb_sb", [P, K, 2 * H])
        w2_sb = sb("w2_sb", [P, E, LAT])
        sq_raw = sb("sq_raw", [P, K, H])
        wgu_raw = sb("wgu_raw", [P, RAW_TILES, 2, K, P])
        wd_raw = sb("wd_raw", [P, FT, H])
        w1_raw = tw_sb[:].rearrange("p n k h -> p (n k h)").rearrange("p (e f) -> p e f", e=E)
        early = sb("early", [P, 2 * E * FFN], F32R)
        wqkv_hi = early[:, 0:K * QKV].rearrange("p (k m) -> p k m", k=K)
        wqkv_lo = early[:, K * QKV:2 * K * QKV].rearrange("p (k m) -> p k m", k=K)
        xg_lo = early[:, 2 * K * QKV:2 * K * QKV + 3 * K * S].rearrange("p (r k s) -> p r k s", r=3, k=K)
        wo_hi, wo_lo = sb("wo_hi", [P, K, H], F32R), sb("wo_lo", [P, K, H], F32R)
        wgu_hi, wgu_lo = sb("wgu_hi", [P, FT, 2, K, P], F32R), sb("wgu_lo", [P, FT, 2, K, P], F32R)
        wd_hi, wd_lo = sb("wd_hi", [P, FT, H], F32R), sb("wd_lo", [P, FT, H], F32R)
        w1_hi, w1_lo = (early[:, c * E * FFN:(c + 1) * E * FFN].rearrange("p (e f) -> p e f", e=E) for c in range(2))
        outw_hi, outw_lo = sb("outw_hi", [P, K, H], F32R), sb("outw_lo", [P, K, H], F32R)
        negid = sb("negid", [P, P], BF16)
        avg = sb("avg", [P, P])
        ones = sb("ones", [P, HD])
        gain1 = sb("gain1", [P, K, B])
        gain2 = sb("gain2", [P, K, B])
        scond = sb("scond", [P, K, B])
        eps_sb = sb("eps_sb", [P, 2])
        shiftb = sb("shiftb", [P, 2 * K, B])
        lnA = sb("lnA", [P, K, B])
        lnB = sb("lnB", [P, K, B])
        posf = sb("posf", [P, B])
        ang = sb("ang", [P, B * FR])
        prob = sb("prob", [P, 2, NH, S])
        first = prob[:].rearrange("p a h s -> p (a h s)")
        turn, whole, *red = (first[:, c * 2 * B * FR:(c + 1) * 2 * B * FR].rearrange("p (c n) -> p c n", c=2)
                             for c in range(5))
        wqkv_raw = first[:, 10 * B * FR:10 * B * FR + K * QKV].rearrange("p (k m) -> p k m", k=K)
        trig = sb("trig", [P, 2, B, FR])
        cs = sb("cs", [P, 2, B, FR])
        ms1 = sb("ms1", [P, B])
        ln1 = sb("ln1", [P, B])
        rstd1 = sb("rstd1", [P, B])
        xg_hi = sb("xg_hi", [P, 3, K, S], F32R)
        ropeA, ropeB = sb("ropeA", [P, QK]), sb("ropeB", [P, QK])
        qk = sb("qk", [P, 2, NH + 1, HD])
        stack = sb("stack", [P, 2, NH + 1, 3, HD])
        qkT = sb("qkT", [P, 2, NH, S], F32R)
        kT = sb("kT", [P, 2, S], F32R)
        v_sb = sb("v_sb", [P, B, HD])
        top = sb("top", [P, 2, NH], BF16)
        rden = sb("rden", [P, K, S])
        ctxn = sb("ctxn", [P, 2, K, S])
        ctx_hi, ctx_lo = sb("ctx_hi", [P, K, HT], F32R), sb("ctx_lo", [P, K, HT], F32R)
        lnrow = sb("lnrow", [P, HT])
        rstd = sb("rstd", [P, HT])
        sqsum = sb("sqsum", [P, HT])
        h_hi, h_lo = sb("h_hi", [P, K, HT], F32R), sb("h_lo", [P, K, HT], F32R)
        act = sb("act", [P, 2, HT])
        act_hi, act_lo = sb("act_hi", [P, FT, HT], F32R), sb("act_lo", [P, FT, HT], F32R)
        hf = xn_sb[:, 0:NB, :].rearrange("p b h -> p (b h)").rearrange("p (k t) -> p k t", k=K)
        sq = xn_sb[:, NB:B, :].rearrange("p b h -> p (b h)").rearrange("p (k t) -> p k t", k=K)
        s4, sq4, h4_hi, h4_lo = (a.rearrange("p k t -> p (k t)").rearrange("p (c k t) -> p c k t", c=2, k=K)
                                 for a in (hf, sq, h_hi[:], h_lo[:]))
        hid = [half_e[:, e] for half_e in (
            wgu_raw[:].rearrange("p f g k m -> p (f g k m)").rearrange("p (e c t) -> p e c t", e=HG, c=2),
            first.rearrange("p (e c t) -> p e c t", e=HG, c=2)) for e in range(HG)]
        yln = wd_raw[:].rearrange("p f h -> p (f h)").rearrange("p (c i k t) -> p c i k t", c=2, i=2, k=K)
        x3_hi, x3_lo = (a[:, 0:K * HALVES].rearrange("p f t -> p (f t)").rearrange("p (k t) -> p k t", k=K)
                        for a in (act_hi, act_lo))

        def act_part(part, n, f):
            if n == 0:
                return (act_hi, act_lo)[part][:, f]
            return (wgu_hi, wgu_lo)[part][:, f].rearrange("p g k m -> p (g k m)")

        bank = [ctx.enter_context(nc.psum_tensor(f"bank{i}", [P, 512], F32)) for i in range(8)]
        proj_ps, ctx_ps = bank[0], bank[1]
        score_ps = bank[4:6]

        def pair(b):
            return bank[6:8] if b % 2 else bank[2:4]

        gate_ps, up_ps = bank[2], bank[3]
        down_ps = bank[6:8]
        attn_out_ps = ((bank[0], bank[0]), (bank[4], bank[5]))
        ms2_ps = (bank[0], bank[4])
        expert_in_ps = (bank[0], bank[6], bank[7])
        expert_out_ps, mean_ps, var_ps, last_ps = bank[4], bank[5], bank[2], bank[1]

        ld = {n: sem("ld_" + n) for n in (
            "small", "ident", "pos", "tw1", "tw2", "xT0", "xT1", "xn0", "xn1", "wqkv", "wo", "wgu0", "wgu1",
            "wgu2", "wgu3", "wd", "w1", "w2", "embw", "outw")}
        eps_ready = sem("eps_ready")
        zeroed, consts_ready, negid_ready = sem("zeroed"), sem("consts_ready"), sem("negid_ready")
        wqkv_split, weight_hi, weight_lo = sem("wqkv_split"), sem("weight_hi"), sem("weight_lo")
        scale1_done, gain1_done = sem("scale1_done"), sem("gain1_done")
        scale2_done, gain2_done = sem("scale2_done"), sem("gain2_done")
        scond_done, emb_done, shift_done, lnab_done = (
            sem("scond_done"), sem("emb_done"), sem("shift_done"), sem("lnab_done"))
        table_step, trig_done, ms1_done, ln1_done, rstd1_done, cs_done = (
            sem("table_step"), sem("trig_done"), sem("ms1_done"), sem("ln1_done"), sem("rstd1_done"), sem("cs_done"))
        xg_hi_done, xg_lo_done, proj_done = sem("xg_hi_done"), sem("xg_lo_done"), sem("proj_done")
        rope_mul, rope_done, v_done = sem("rope_mul"), sem("rope_done"), sem("v_done")
        qk_hi_done, qk_lo_done = sem("qk_hi_done"), sem("qk_lo_done")
        turned, kturned, qT_done, kT_done = sem("turned"), sem("kturned"), sem("qT_done"), sem("kT_done")
        s1_done, top_done, st_done, exp_done = sem("s1_done"), sem("top_done"), sem("st_done"), sem("exp_done")
        pv_done, lden_done, rden_done, ctxn_done = (
            sem("pv_done"), sem("lden_done"), sem("rden_done"), sem("ctxn_done"))
        ctx_hi_done, ctx_lo_done = sem("ctx_hi_done"), sem("ctx_lo_done")
        wo_done, x2_done = sem("wo_done"), sem("x2_done")
        sq2_done, sqsum2_done, ms2_done, ln2_done, rstd2_done = (
            sem("sq2_done"), sem("sqsum2_done"), sem("ms2_done"), sem("ln2_done"), sem("rstd2_done"))
        h_done, h_hi_done, h_lo_done = sem("h_done"), sem("h_hi_done"), sem("h_lo_done")
        gate_mm, up_mm, gate_done, act_done = sem("gate_mm"), sem("up_mm"), sem("gate_done"), sem("act_done")
        act_hi_done, act_lo_done = sem("act_hi_done"), sem("act_lo_done")
        down_done, x3_done, x3_hi_done, x3_lo_done = (
            sem("down_done"), sem("x3_done"), sem("x3_hi_done"), sem("x3_lo_done"))
        e1_done, gelu_done, e2_done, y_done = sem("e1_done"), sem("gelu_done"), sem("e2_done"), sem("y_done")
        ysum_done, mean_done, dev_done, sqd_done, sqdsum_done, var_done, lnv_done, rstdv_done = (
            sem("ysum_done"), sem("mean_done"), sem("dev_done"), sem("sqd_done"), sem("sqdsum_done"),
            sem("var_done"), sem("lnv_done"), sem("rstdv_done"))
        z_done, s_done, s_hi_done, s_lo_done = sem("z_done"), sem("s_done"), sem("s_hi_done"), sem("s_lo_done")
        out_mm, fin_done, stored = sem("out_mm"), sem("fin_done"), sem("stored")

        W_WO, W_GU, W_D, W_1, W_OUT = 1, 2, 2 + FT, 2 + 2 * FT, 4 + 2 * FT
        block = ctx.enter_context(nc.Block())

        def half(n):
            return slice(n * HT, (n + 1) * HT)

        def quarter(c):
            return slice(c * QT, (c + 1) * QT)

        def tok(b):
            return slice(b % NB * S, (b % NB + 1) * S)

        @block.sync
        def _(sp):
            sp.dma_start(small_sb[:], small).then_inc(ld["small"], 16)
            sp.dma_start(tw1_sb[:], tw1).then_inc(ld["tw1"], 16)
            sp.dma_start(pos_sb[:], posT).then_inc(ld["pos"], 16)
            sp.dma_start(xn_sb[:, 0:NB], xn[:, 0:NB]).then_inc(ld["xn0"], 16)
            sp.dma_start(res_sb[:, :, half(0)], xT[:, :, half(0)]).then_inc(ld["xT0"], 16)
            sp.dma_start(wqkv_raw, wqkv).then_inc(ld["wqkv"], 16)
            sp.dma_start(id_sb[:], ident).then_inc(ld["ident"], 16)
            sp.dma_start(sq_raw[:], wo).then_inc(ld["wo"], 16)
            sp.dma_start(xn_sb[:, NB:B], xn[:, NB:B]).then_inc(ld["xn1"], 16)
            sp.dma_start(res_sb[:, :, half(1)], xT[:, :, half(1)]).then_inc(ld["xT1"], 16)
            sp.dma_start(tw2_sb[:], tw2).then_inc(ld["tw2"], 16)
            for c in range(4):
                if c == 2:
                    sp.dma_start(wd_raw[:], wd).then_inc(ld["wd"], 16)
                if c >= 2:
                    sp.wait_ge(weight_lo, W_GU + 2 * c - 3)
                r = 2 * c % RAW_TILES
                sp.dma_start(wgu_raw[:, r:r + 2], wgu[:, 2 * c:2 * c + 2]).then_inc(ld[f"wgu{c}"], 16)
            sp.wait_ge(zeroed, 1)
            for r in range(4):
                sp.dma_start(w1_raw[32 * r:32 * r + 32, r::4], w1[:, r::4]).then_inc(ld["w1"], 16)
            sp.dma_start(emb_sb[:], embw).then_inc(ld["embw"], 16)
            sp.dma_start(w2_sb[:], w2).then_inc(ld["w2"], 16)
            sp.dma_start(sq_raw[:], outw).then_inc(ld["outw"], 16)
            for c in range(QUARTERS):
                sp.wait_ge(fin_done, K * (c + 1))
                sp.dma_start(out[:, :, quarter(c)], res_sb[:, :, quarter(c)]).then_inc(stored, 16)
            sp.wait_ge(stored, 16 * QUARTERS)

        @block.gpsimd
        def _(pool):
            nc.gpsimd.memset(avg[:], 1.0 / H).then_inc(consts_ready, 1)
            nc.gpsimd.memset(ones[:], 1.0).then_inc(consts_ready, 1)

            def split(raw, hi, lo, loads):
                for s, n in loads:
                    pool.wait_ge(s, n)
                nc.gpsimd.tensor_copy(hi, raw).then_inc(weight_hi, 1)
                split.n += 1
                pool.wait_ge(weight_hi, split.n)
                nc.gpsimd.tensor_tensor(lo, raw, hi.bitcast(F32), ALU.subtract).then_inc(weight_lo, 1)
            split.n = 0
            split(sq_raw[:], wo_hi[:], wo_lo[:], [(ld["wo"], 16)])
            pool.wait_ge(scale1_done, 1)
            pool.wait_ge(scale2_done, 1)
            nc.gpsimd.memset(w1_raw, 0.0).then_inc(zeroed, 1)
            for f in range(FT):
                split(wgu_raw[:, f % RAW_TILES], wgu_hi[:, f], wgu_lo[:, f], [(ld[f"wgu{f // 2}"], 16)])

            def act_low(n, f):
                pool.wait_ge(act_hi_done, FT * n + f + 1)
                nc.gpsimd.tensor_tensor(act_part(1, n, f), act[:, f % 2], act_part(0, n, f).bitcast(F32),
                                        ALU.subtract).then_inc(act_lo_done, 1)
            for f in range(FT):
                split(wd_raw[:, f], wd_hi[:, f], wd_lo[:, f], [(ld["wd"], 16)])
            pool.wait_ge(proj_done, B)
            for c in range(2):
                split(w1_raw[:, 4 * c:4 * c + 4], w1_hi[:, 4 * c:4 * c + 4], w1_lo[:, 4 * c:4 * c + 4], [(ld["w1"], 64)])
            split(sq_raw[:], outw_hi[:], outw_lo[:], [(ld["outw"], 16)])
            for n in range(HALVES):
                for f in range(FT):
                    act_low(n, f)

        @block.scalar
        def _(act_e):
            A = nc.scalar.activation

            def mean_square(n):
                act_e.wait_ge(ld[f"xn{n}"], 16)
                if n:
                    act_e.wait_ge(ms1_done, NB * n)
                for b in range(NB * n, NB * n + NB):
                    A(sq_junk(b), xn_sb[:, b], ACT.Square, accum_out=ms1[:, b:b + 1]).then_inc(ms1_done, 1)

            def sq_junk(b):
                return act[:].rearrange("p a t -> p (a t)")[:, b % NB * H:(b % NB + 1) * H]

            def rstd_first(n):
                bs = slice(NB * n, NB * n + NB)
                act_e.wait_ge(ms1_done, NB * n + NB)
                A(ln1[:, bs], ms1[:, bs], ACT.Ln, scale=1.0 / H, bias=eps_rms).then_inc(ln1_done, 1)
                act_e.wait_ge(ln1_done, n + 1)
                A(rstd1[:, bs], ln1[:, bs], ACT.Exp, scale=-0.5).then_inc(rstd1_done, 1)

            eps_rms, eps_ln = eps_sb[:, 0:1], eps_sb[:, 1:2]

            def xg_high(b):
                act_e.wait_ge(ld[f"xT{b // NB}"], 16)
                act_e.wait_ge(gain1_done, K)
                if b >= 3:
                    act_e.wait_ge(proj_done, b - 2)
                for k in range(K):
                    A(xg_hi[:, b % 3, k], res_sb[:, k, b * S:(b + 1) * S], ACT.Copy,
                      scale=gain1[:, k, b:b + 1]).then_inc(xg_hi_done, 1)

            def stack_high(b):
                act_e.wait_ge(rope_done, 2 * (b + 1))
                if b >= 2:
                    act_e.wait_ge(turned, 2 * (b - 1))
                    act_e.wait_ge(kturned, b - 1)
                st = stack[:, b % 2].bitcast(F32R)
                A(st[:, 0:NH, 0::2], qk[:, b % 2, 0:NH].rearrange("p h (c d) -> p h c d", c=1).broadcast_to([P, NH, 2, HD]),
                  ACT.Copy).then_inc(qk_hi_done, 1)
                A(st[:, NH, 0:2], qk[:, b % 2, NH:NH + 1].broadcast_to([P, 2, HD]), ACT.Copy).then_inc(qk_hi_done, 1)

            def take_turned(b):
                if b >= 2:
                    act_e.wait_ge(st_done, 2 * (b - 1))
                for g in range(2):
                    act_e.wait_ge(turned, 2 * b + g + 1)
                    A(qkT[0:96, b % 2, HG * g:HG * g + HG].rearrange("p h s -> p (h s)"), pair(b)[g][0:96, :],
                      ACT.Copy).then_inc(qT_done, 1)
                act_e.wait_ge(kturned, b + 1)
                A(kT[0:96, b % 2], score_ps[0][0:96, 0:S], ACT.Copy).then_inc(kT_done, 1)

            def exps(b):
                if b >= 2:
                    act_e.wait_ge(pv_done, b - 1)
                for g in range(2):
                    act_e.wait_ge(st_done, 2 * b + g + 1)
                    A(prob[:, b % 2, HG * g:HG * g + HG].rearrange("p h s -> p (h s)"), pair(b)[g][:, :], ACT.Exp,
                      scale=HD ** -0.5).then_inc(exp_done, 1)

            def reciprocal_of_sum(b):
                act_e.wait_ge(pv_done, b + 1)
                if b >= 1:
                    act_e.wait_ge(ctxn_done, b)
                A(rden[:], ctx_ps[:, K * S:2 * K * S].rearrange("p (k s) -> p k s", k=K), ACT.Ln).then_inc(lden_done, 1)
                act_e.wait_ge(lden_done, b + 1)
                A(rden[:], rden[:], ACT.Exp, scale=-1.0).then_inc(rden_done, 1)

            def ctx_high(b):
                act_e.wait_ge(ctxn_done, b + 1)
                if b == NB:
                    act_e.wait_ge(wo_done, K)
                A(ctx_hi[:, :, tok(b)], ctxn[:, b % 2], ACT.Copy).then_inc(ctx_hi_done, 1)

            def x2_squares(n):
                for k in range(K):
                    act_e.wait_ge(x2_done, K * n + k + 1)
                    if n:
                        act_e.wait_ge(sqsum2_done, n)
                    A(sq[:, k], res_sb[:, k, half(n)], ACT.Square).then_inc(sq2_done, 1)

            def rstd_second(n):
                act_e.wait_ge(ms2_done, n + 1)
                if n:
                    act_e.wait_ge(h_done, NB * K * n)
                A(lnrow[:], ms2_ps[n][:, :], ACT.Ln, bias=eps_rms).then_inc(ln2_done, 1)
                act_e.wait_ge(ln2_done, n + 1)
                A(rstd[:], lnrow[:], ACT.Exp, scale=-0.5).then_inc(rstd2_done, 1)

            def h_high(n):
                act_e.wait_ge(h_done, NB * K * (n + 1))
                if n:
                    act_e.wait_ge(up_mm, FT * n)
                A(h_hi[:], hf, ACT.Copy).then_inc(h_hi_done, 1)

            def silu(n, f):
                i = FT * n + f
                act_e.wait_ge(gate_mm, i + 1)
                if i >= 2:
                    act_e.wait_ge(act_hi_done, i - 1)
                    act_e.wait_ge(act_lo_done, i - 1)
                A(act[:, i % 2], gate_ps[:, :], ACT.Silu).then_inc(gate_done, 1)

            def act_high(n, f):
                i = FT * n + f
                act_e.wait_ge(act_done, i + 1)
                A(act_part(0, n, f), act[:, i % 2], ACT.Copy).then_inc(act_hi_done, 1)

            def x3_high(n):
                for m in range(K):
                    act_e.wait_ge(x3_done, K * n + m + 1)
                    A(x3_hi[:, m, half(n)], res_sb[:, m, half(n)], ACT.Copy).then_inc(x3_hi_done, 1)

            def gelu(c):
                for e in range(E):
                    act_e.wait_ge(e1_done, E // 2 * c + e // 2 + 1)
                    if c >= 2:
                        act_e.wait_ge(e2_done, c - 1)
                    A(hid[e][:, c % 2], expert_in_ps[(E // 2 * c + e // 2) % 3][:, e % 2 * QT:(e % 2 + 1) * QT], ACT.Gelu,
                      bias=small_sb[:, C_B1 + e:C_B1 + e + 1]).then_inc(gelu_done, 1)

            def norm_squares(c):
                act_e.wait_ge(dev_done, c + 1)
                if c >= 2:
                    act_e.wait_ge(sqdsum_done, c - 1)
                A(sq4[:, c % 2], yln[:, c % 2, 1], ACT.Square).then_inc(sqd_done, 1)

            def row(a, c):
                return a[:, c % 2 * QT:(c % 2 + 1) * QT]

            def norm_rstd(c):
                act_e.wait_ge(var_done, c + 1)
                if c >= 2:
                    act_e.wait_ge(z_done, c - 1)
                A(row(lnrow, c), var_ps[:, 0:QT], ACT.Ln, bias=eps_ln).then_inc(lnv_done, 1)
                act_e.wait_ge(lnv_done, c + 1)
                A(row(rstd, c), row(lnrow, c), ACT.Exp, scale=-0.5).then_inc(rstdv_done, 1)

            def norm_silu(c):
                act_e.wait_ge(lnab_done, 3)
                act_e.wait_ge(z_done, c + 1)
                if c >= 2:
                    act_e.wait_ge(s_lo_done, c - 1)
                for k in range(K):
                    for j in range(QS):
                        b = QS * c + j
                        A(s4[:, c % 2, k, j * S:(j + 1) * S], yln[:, c % 2, 0, k, j * S:(j + 1) * S], ACT.Silu,
                          scale=lnA[:, k, b:b + 1], bias=lnB[:, k, b:b + 1]).then_inc(s_done, 1)

            def s_high(c):
                act_e.wait_ge(s_done, QS * K * (c + 1))
                if c >= 2:
                    act_e.wait_ge(out_mm, c - 1)
                else:
                    act_e.wait_ge(up_mm, 2 * FT)
                A(h4_hi[:, c % 2], s4[:, c % 2], ACT.Copy).then_inc(s_hi_done, 1)

            def table(name):
                nc.scalar.preload_act_table_set(name)

            mean_square(0)
            act_e.wait_ge(table_step, TABLE_READY)
            A(trig[:].rearrange("p c b f -> p (c b f)"), red[2].rearrange("p c n -> p (c n)"),
              ACT.Sin).then_inc(trig_done, 1)
            table("natural_log_exp_and_others")
            act_e.wait_ge(eps_ready, 2)
            xg_high(0)
            rstd_first(0)
            xg_high(1)
            stack_high(0)
            xg_high(2)
            take_turned(0)
            stack_high(1)
            mean_square(1)
            rstd_first(1)
            for b in range(B):
                if b >= 1:
                    reciprocal_of_sum(b - 1)
                if b + 1 < B:
                    take_turned(b + 1)
                exps(b)
                if b == NB + 2:
                    ctx_high(NB)
                if b >= 1 and b != NB + 1:
                    ctx_high(b - 1)
                if b + 2 < B:
                    stack_high(b + 2)
                if b + 3 < B:
                    xg_high(b + 3)
                if b == 6:
                    x2_squares(0)
                if b == 7:
                    rstd_second(0)
            reciprocal_of_sum(B - 1)
            h_high(0)
            ctx_high(B - 1)
            table("silu_and_others")
            act_e.wait_ge(ld["small"], 16)
            A(scond[:].rearrange("p k b -> p (k b)"), small_sb[:, C_COND:C_COND + K * B], ACT.Silu).then_inc(scond_done, 1)
            for f in range(FT):
                silu(0, f)
                act_high(0, f)
                if f == 2:
                    x2_squares(1)
            table("natural_log_exp_and_others")
            rstd_second(1)
            h_high(1)
            for f in range(FT):
                silu(1, f)
                act_high(1, f)
                if f == 6:
                    x3_high(0)
            gelu(0)
            gelu(1)
            norm_squares(0)
            norm_squares(1)
            table("natural_log_exp_and_others")
            norm_rstd(0)
            norm_rstd(1)
            table("silu_and_others")
            norm_silu(0)
            s_high(0)
            norm_silu(1)
            s_high(1)
            x3_high(1)
            gelu(2)
            gelu(3)
            norm_squares(2)
            norm_squares(3)
            table("natural_log_exp_and_others")
            norm_rstd(2)
            norm_rstd(3)
            table("silu_and_others")
            norm_silu(2)
            s_high(2)
            norm_silu(3)
            s_high(3)

        @block.vector
        def _(dve):
            TT, TS, STT = nc.vector.tensor_tensor, nc.vector.tensor_scalar, nc.vector.scalar_tensor_tensor

            def col(c, n=1):
                return small_sb[:, c:c + n]

            nc.vector.memset(eps_sb[:, 0:1], RMS_EPS).then_inc(eps_ready, 1)
            nc.vector.memset(eps_sb[:, 1:2], LN_EPS).then_inc(eps_ready, 1)

            def rotary_tables():
                dve.wait_ge(ld["pos"], 16)
                dve.wait_ge(ld["small"], 16)
                n = [0]

                def then(ins):
                    n[0] += 1
                    ins.then_inc(table_step, 1)
                    dve.wait_ge(table_step, n[0])
                both = [P, 2, B * FR]
                then(nc.vector.tensor_copy(posf[:], pos_sb[:]))
                then(TT(ang[:].rearrange("p (b f) -> p b f", b=B),
                        posf[:].rearrange("p (b f) -> p b f", f=1).broadcast_to([P, B, FR]),
                        col(C_INVF, FR).rearrange("p (b f) -> p b f", b=1).broadcast_to([P, B, FR]), ALU.mult))
                then(TS(turn[:, 0], ang[:], 0.5 / PI, 0.25, ALU.mult, ALU.add))
                then(TS(turn[:, 1], ang[:], 0.5 / PI, None, ALU.mult))
                then(TS(whole, turn, MAGIC, -MAGIC, ALU.add, ALU.add))
                then(STT(red[0], whole, -TAU_A, ang[:].rearrange("p (c n) -> p c n", c=1).broadcast_to(both),
                         ALU.mult, ALU.add))
                then(STT(red[1], whole, -TAU_B, red[0], ALU.mult, ALU.add))
                then(STT(red[0], whole, -TAU_C, red[1], ALU.mult, ALU.add))
                then(TS(red[0][:, 0], red[0][:, 0], PI / 2, None, ALU.add))
                TS(red[2], red[0], 3.1415925, -3.1415925, ALU.min, ALU.max).then_inc(table_step, 1)
                assert n[0] + 1 == TABLE_READY

            def scaled_table(n):
                dve.wait_ge(trig_done, 1)
                dve.wait_ge(rstd1_done, n + 1)
                for c in range(2):
                    bs = slice(NB * n, NB * n + NB)
                    TT(cs[:, c, bs], trig[:, c, bs],
                       rstd1[:, bs].rearrange("p (b f) -> p b f", f=1).broadcast_to([P, NB, FR]),
                       ALU.mult).then_inc(cs_done, 1)

            def gains(ps, w_col, gain, mm_done, done):
                dve.wait_ge(mm_done, 1)
                for m in range(K):
                    TS(gain[:, m], ps[:, m * B:(m + 1) * B], 1.0, col(w_col + m), ALU.add, ALU.mult).then_inc(done, 1)

            def xg_low(b):
                for k in range(K):
                    dve.wait_ge(xg_hi_done, K * b + k + 1)
                    if b >= 3 and k == 0:
                        dve.wait_ge(proj_done, b - 2)
                    STT(xg_lo[:, b % 3, k], res_sb[:, k, b * S:(b + 1) * S], gain1[:, k, b:b + 1],
                        xg_hi[:, b % 3, k].bitcast(F32), ALU.mult, ALU.subtract).then_inc(xg_lo_done, 1)

            def rope(b):
                dve.wait_ge(proj_done, b + 1)
                dve.wait_ge(cs_done, 2 * (b // NB + 1))
                if b >= 1:
                    dve.wait_ge(rope_done, 2 * b)
                heads = [P, 2 * (NH + 1), FR]
                for c, o in ((0, ropeA), (1, ropeB)):
                    TT(o[:].rearrange("p (h f) -> p h f", f=FR), proj_ps[:, 0:QK].rearrange("p (h f) -> p h f", f=FR),
                       cs[:, c, b:b + 1].broadcast_to(heads), ALU.mult).then_inc(rope_mul, 1)
                TS(v_sb[:, b], proj_ps[:, QK:QKV], rstd1[:, b:b + 1], None, ALU.mult).then_inc(v_done, 1)
                a = ropeA[:].rearrange("p (h c f) -> p h c f", c=2, f=FR)
                s = ropeB[:].rearrange("p (h c f) -> p h c f", c=2, f=FR)
                dve.wait_ge(rope_mul, 2 * (b + 1))
                if b >= 2:
                    dve.wait_ge(qk_hi_done, 2 * (b - 1))
                    dve.wait_ge(qk_lo_done, 2 * (b - 1))
                TT(qk[:, b % 2, :, 0:FR], a[:, :, 0], s[:, :, 1], ALU.subtract).then_inc(rope_done, 1)
                TT(qk[:, b % 2, :, FR:HD], a[:, :, 1], s[:, :, 0], ALU.add).then_inc(rope_done, 1)

            def stack_low(b):
                dve.wait_ge(rope_done, 2 * (b + 1))
                dve.wait_ge(qk_hi_done, 2 * (b + 1))
                if b >= 2:
                    dve.wait_ge(turned, 2 * (b - 1))
                    dve.wait_ge(kturned, b - 1)
                st = stack[:, b % 2]
                TT(st[:, 0:NH, 1].bitcast(F32R), qk[:, b % 2, 0:NH], st[:, 0:NH, 0], ALU.subtract).then_inc(qk_lo_done, 1)
                TT(st[:, NH, 2].bitcast(F32R), qk[:, b % 2, NH], st[:, NH, 0], ALU.subtract).then_inc(qk_lo_done, 1)

            def maxima(b):
                if b >= 2:
                    dve.wait_ge(st_done, 2 * (b - 1))
                dve.wait_ge(s1_done, 2 * (b + 1))
                for g in range(2):
                    nc.vector.tensor_reduce(top[:, b % 2, HG * g:HG * g + HG],
                                            score_ps[g][:, :].rearrange("p (h t) -> p h t", h=HG),
                                            AX.X, ALU.max).then_inc(top_done, 1)

            def context(b):
                dve.wait_ge(rden_done, b + 1)
                if b >= 2:
                    dve.wait_ge(ctx_hi_done, b - 1)
                    dve.wait_ge(ctx_lo_done, b - 1)
                TT(ctxn[:, b % 2], ctx_ps[:, 0:K * S].rearrange("p (k s) -> p k s", k=K), rden[:],
                   ALU.mult).then_inc(ctxn_done, 1)

            def context_low(b):
                dve.wait_ge(ctx_hi_done, b + 1)
                if b == NB:
                    dve.wait_ge(wo_done, K)
                TT(ctx_lo[:, :, tok(b)], ctxn[:, b % 2], ctx_hi[:, :, tok(b)].bitcast(F32),
                   ALU.subtract).then_inc(ctx_lo_done, 1)

            def x2(n, tiles=range(K)):
                for m in tiles:
                    dve.wait_ge(wo_done, K * n + m + 1)
                    r = res_sb[:, m, half(n)]
                    TT(r, attn_out_ps[n][m][:, :], r, ALU.add).then_inc(x2_done, 1)

            def square_sum(n):
                dve.wait_ge(sq2_done, K * (n + 1))
                TT(sqsum[:], sq[:, 0], sq[:, 1], ALU.add).then_inc(sqsum2_done, 1)

            def normed(n):
                dve.wait_ge(rstd2_done, n + 1)
                dve.wait_ge(gain2_done, K)
                for k in range(K):
                    for j in range(NB):
                        b = NB * n + j
                        STT(hf[:, k, j * S:(j + 1) * S], res_sb[:, k, b * S:(b + 1) * S], gain2[:, k, b:b + 1],
                            rstd[:, j * S:(j + 1) * S], ALU.mult, ALU.mult).then_inc(h_done, 1)

            def normed_low(n):
                dve.wait_ge(h_hi_done, n + 1)
                if n:
                    dve.wait_ge(up_mm, FT * n)
                TT(h_lo[:], hf, h_hi[:].bitcast(F32), ALU.subtract).then_inc(h_lo_done, 1)

            def gated(n, f):
                i = FT * n + f
                dve.wait_ge(gate_done, i + 1)
                dve.wait_ge(up_mm, i + 1)
                TT(act[:, i % 2], up_ps[:, :], act[:, i % 2], ALU.mult).then_inc(act_done, 1)

            def x3(n):
                for m in range(K):
                    dve.wait_ge(down_done, K * n + m + 1)
                    r = res_sb[:, m, half(n)]
                    TT(r, down_ps[m][:, :], r, ALU.add).then_inc(x3_done, 1)

            def x3_low(n):
                for m in range(K):
                    dve.wait_ge(x3_hi_done, K * n + m + 1)
                    TT(x3_lo[:, m, half(n)], res_sb[:, m, half(n)], x3_hi[:, m, half(n)].bitcast(F32),
                       ALU.subtract).then_inc(x3_lo_done, 1)

            def row(a, c):
                return a[:, c % 2 * QT:(c % 2 + 1) * QT]

            def expert_out(c):
                dve.wait_ge(e2_done, c + 1)
                if c >= 2:
                    dve.wait_ge(s_done, QS * K * (c - 1))
                    dve.wait_ge(var_done, c - 1)
                for g in range(K):
                    TS(yln[:, c % 2, 0, g], expert_out_ps[:, g * QT:(g + 1) * QT], col(C_B2 + g), None,
                       ALU.add).then_inc(y_done, 1)
                dve.wait_ge(y_done, K * (c + 1))
                TT(row(sqsum, c), yln[:, c % 2, 0, 0], yln[:, c % 2, 0, 1], ALU.add).then_inc(ysum_done, 1)

            def centred(c):
                dve.wait_ge(mean_done, c + 1)
                if c >= 2:
                    dve.wait_ge(z_done, c - 1)
                TT(yln[:, c % 2, 1], yln[:, c % 2, 0],
                   mean_ps[:, 0:QT].rearrange("p (k t) -> p k t", k=1).broadcast_to([P, K, QT]),
                   ALU.subtract).then_inc(dev_done, 1)

            def dev_sum(c):
                dve.wait_ge(sqd_done, c + 1)
                TT(row(sqsum, c), sq4[:, c % 2, 0], sq4[:, c % 2, 1], ALU.add).then_inc(sqdsum_done, 1)

            def standard(c):
                dve.wait_ge(rstdv_done, c + 1)
                TT(yln[:, c % 2, 0], yln[:, c % 2, 1],
                   row(rstd, c).rearrange("p (k t) -> p k t", k=1).broadcast_to([P, K, QT]),
                   ALU.mult).then_inc(z_done, 1)

            def s_low(c):
                dve.wait_ge(s_hi_done, c + 1)
                if c >= 2:
                    dve.wait_ge(out_mm, c - 1)
                TT(h4_lo[:, c % 2], s4[:, c % 2], h4_hi[:, c % 2].bitcast(F32), ALU.subtract).then_inc(s_lo_done, 1)

            def finish(c):
                dve.wait_ge(out_mm, c + 1)
                for m in range(K):
                    r = res_sb[:, m, quarter(c)]
                    STT(r, last_ps[:, m * QT:(m + 1) * QT], col(C_OUTB + m), r, ALU.add, ALU.add).then_inc(fin_done, 1)

            def layer_norm_affine():
                dve.wait_ge(emb_done, 1)
                for m in range(2 * K):
                    TS(shiftb[:, m], last_ps[:, m * B:(m + 1) * B], col(C_EMBB + m), None, ALU.add).then_inc(shift_done, 1)
                dve.wait_ge(shift_done, 2 * K)
                for m in range(K):
                    TS(lnA[:, m], shiftb[:, m], 1.0, col(C_LNG + m), ALU.add, ALU.mult).then_inc(shift_done, 1)
                    TS(lnB[:, m], shiftb[:, m], 1.0, col(C_LNB + m), ALU.add, ALU.mult).then_inc(shift_done, 1)
                dve.wait_ge(shift_done, 4 * K)
                TT(lnB[:], lnB[:], shiftb[:, K:2 * K], ALU.add).then_inc(lnab_done, 3)

            rotary_tables()
            gains(bank[7], C_LN1W, gain1, scale1_done, gain1_done)
            dve.wait_ge(ld["wqkv"], 16)
            nc.vector.tensor_copy(wqkv_hi, wqkv_raw).then_inc(wqkv_split, 1)
            dve.wait_ge(wqkv_split, 1)
            TT(wqkv_lo, wqkv_raw, wqkv_hi.bitcast(F32), ALU.subtract).then_inc(wqkv_split, 1)
            dve.wait_ge(gain1_done, K)
            xg_low(0)
            scaled_table(0)
            rope(0)
            xg_low(1)
            stack_low(0)
            gains(bank[6], C_LN2W, gain2, scale2_done, gain2_done)
            dve.wait_ge(ld["ident"], 16)
            TS(negid[:], id_sb[:], -1.0, None, ALU.mult).then_inc(negid_ready, 1)
            rope(1)
            xg_low(2)
            stack_low(1)
            maxima(0)
            scaled_table(1)
            for b in range(B):
                if b >= 1:
                    context(b - 1)
                if b == 5:
                    x2(0, [0])
                if b == 6:
                    x2(0, [1])
                if b + 2 < B:
                    rope(b + 2)
                if b == NB + 2:
                    context_low(NB)
                if b >= 1 and b != NB + 1:
                    context_low(b - 1)
                if b + 1 < B:
                    maxima(b + 1)
                if b + 3 < B:
                    xg_low(b + 3)
                if b + 2 < B:
                    stack_low(b + 2)
                if b == 6:
                    square_sum(0)
            normed(0)
            context(B - 1)
            normed_low(0)
            context_low(B - 1)
            for f in range(FT):
                gated(0, f)
                if f == 2:
                    x2(1)
                if f == 3:
                    square_sum(1)
            normed(1)
            normed_low(1)
            for f in range(FT):
                gated(1, f)
                if f == 5:
                    x3(0)
                if f == 6:
                    x3_low(0)
            layer_norm_affine()
            expert_out(0)
            centred(0)
            expert_out(1)
            dev_sum(0)
            centred(1)
            dev_sum(1)
            standard(0)
            standard(1)
            s_low(0)
            x3(1)
            s_low(1)
            x3_low(1)
            finish(0)
            finish(1)
            expert_out(2)
            centred(2)
            expert_out(3)
            dev_sum(2)
            centred(3)
            dev_sum(3)
            standard(2)
            standard(3)
            s_low(2)
            s_low(3)
            finish(2)
            finish(3)

        @block.tensor
        def _(pe):
            MM = nc.tensor.matmul

            def mm3(out_ap, parts, first=True, last=True):
                for i, (lh, ll, rh, rl) in enumerate(parts):
                    MM(out_ap, lh, rh, start=first and i == 0, stop=False)
                    MM(out_ap, lh, rl, start=False, stop=False)
                    mm = MM(out_ap, ll, rh, start=False, stop=last and i == len(parts) - 1)
                return mm

            def scale_of(tw_sb, ps, load, done):
                pe.wait_ge(ld["small"], 16)
                pe.wait_ge(load, 16)
                for m in range(K):
                    for k in range(K):
                        mm = MM(ps[:, m * B:(m + 1) * B], tw_sb[:, k, m * P:(m + 1) * P],
                                small_sb[:, C_COND + k * B:C_COND + (k + 1) * B], start=k == 0, stop=k == K - 1)
                mm.then_inc(done, 1)

            def project(b):
                if b == 0:
                    pe.wait_ge(wqkv_split, 2)
                else:
                    pe.wait_ge(rope_mul, 2 * b)
                    pe.wait_ge(v_done, b)
                pe.wait_ge(xg_hi_done, K * (b + 1))
                pe.wait_ge(xg_lo_done, K * (b + 1))
                mm3(proj_ps[:, 0:QKV], [(xg_hi[:, b % 3, k], xg_lo[:, b % 3, k], wqkv_hi[:, k], wqkv_lo[:, k])
                                        for k in range(K)]).then_inc(proj_done, 1)

            def turn_queries(b):
                pe.wait_ge(qk_hi_done, 2 * (b + 1))
                pe.wait_ge(qk_lo_done, 2 * (b + 1))
                if b == 0:
                    pe.wait_ge(ld["ident"], 16)
                if b == 1:
                    pe.wait_ge(gain1_done, K)
                    pe.wait_ge(gain2_done, K)
                if b >= 2:
                    pe.wait_ge(exp_done, 2 * (b - 1))
                for g in range(2):
                    for h in range(HG):
                        mm = nc.tensor.transpose(pair(b)[g][0:96, h * S:(h + 1) * S],
                                                 stack[:, b % 2, HG * g + h].rearrange("p c d -> p (c d)"), id_sb[:])
                    mm.then_inc(turned, 1)

            def turn_key(b):
                if b >= 1:
                    pe.wait_ge(top_done, 2 * b)
                nc.tensor.transpose(score_ps[0][0:96, 0:S], stack[:, b % 2, NH].rearrange("p c d -> p (c d)"),
                                    id_sb[:]).then_inc(kturned, 1)

            def scores_for_max(b):
                pe.wait_ge(kT_done, b + 1)
                for g in range(2):
                    pe.wait_ge(qT_done, 2 * b + g + 1)
                    for h in range(HG):
                        mm = MM(score_ps[g][:, h * S:(h + 1) * S], qkT[0:96, b % 2, HG * g + h], kT[0:96, b % 2],
                                start=True, stop=True)
                    mm.then_inc(s1_done, 1)

            def scores_transposed(b):
                if b == 0:
                    pe.wait_ge(negid_ready, 1)
                for g in range(2):
                    ps = pair(b)[g]
                    MM(ps[:, :], kT[0:96, b % 2], qkT[0:96, b % 2, HG * g:HG * g + HG].rearrange("p h s -> p (h s)"),
                       start=True, stop=False)
                    pe.wait_ge(top_done, 2 * b + g + 1)
                    for h in range(HG):
                        mm = MM(ps[:, h * S:(h + 1) * S],
                                top[:, b % 2, HG * g + h:HG * g + h + 1].broadcast_to([P, S]), negid[:],
                                start=False, stop=h == HG - 1)
                    mm.then_inc(st_done, 1)

            def weigh_values(b):
                pe.wait_ge(exp_done, 2 * (b + 1))
                pe.wait_ge(v_done, b + 1)
                if b == 0:
                    pe.wait_ge(consts_ready, 2)
                if b >= 1:
                    pe.wait_ge(ctxn_done, b)
                for c, w in ((0, v_sb[:, b]), (1, ones[:])):
                    for r in range(4):
                        mm = MM(ctx_ps[32 * r:32 * r + 32, c * K * S:(c + 1) * K * S], w,
                                prob[:, b % 2, r::4], start=True, stop=True)
                mm.then_inc(pv_done, 1)

            def attn_out(n, m):
                if m == 0:
                    pe.wait_ge(weight_lo, W_WO)
                    pe.wait_ge(ctx_hi_done, NB * (n + 1))
                    pe.wait_ge(ctx_lo_done, NB * (n + 1))
                if n == 0:
                    pe.wait_ge(rope_mul, 2 * (B - 1 + m))
                    pe.wait_ge(v_done, B - 1 + m)
                else:
                    pe.wait_ge(top_done, 2 * B)
                ms = slice(m * P, (m + 1) * P)
                mm3(attn_out_ps[n][m][:, :], [(wo_hi[:, k, ms], wo_lo[:, k, ms], ctx_hi[:, k], ctx_lo[:, k])
                                              for k in range(K)]).then_inc(wo_done, 1)

            def mean_of_squares(n):
                pe.wait_ge(sqsum2_done, n + 1)
                pe.wait_ge(x2_done, K * (n + 1))
                MM(ms2_ps[n][:, :], avg[:], sqsum[:], start=True, stop=True).then_inc(ms2_done, 1)

            def gate_or_up(n, f, u):
                i = FT * n + f
                if f == 0:
                    pe.wait_ge(h_hi_done, n + 1)
                    pe.wait_ge(h_lo_done, n + 1)
                pe.wait_ge(weight_lo, W_GU + f)
                if u == 0:
                    if i:
                        pe.wait_ge(gate_done, i)
                    else:
                        pe.wait_ge(exp_done, 2 * (B - 1))
                elif i:
                    pe.wait_ge(act_done, i)
                mm3((gate_ps, up_ps)[u][:, :], [(wgu_hi[:, f, u, k], wgu_lo[:, f, u, k], h_hi[:, k], h_lo[:, k])
                                                for k in range(K)]).then_inc((gate_mm, up_mm)[u], 1)

            def down(n, m):
                if n:
                    pe.wait_ge(x3_done, m + 1)
                    pe.wait_ge(gelu_done, 2 * E)
                elif m == 0:
                    pe.wait_ge(exp_done, 2 * B)
                ms = slice(m * P, (m + 1) * P)
                for f in range(FT):
                    if m == 0:
                        pe.wait_ge(weight_lo, W_D + f)
                        pe.wait_ge(act_hi_done, FT * n + f + 1)
                        pe.wait_ge(act_lo_done, FT * n + f + 1)
                    mm = mm3(down_ps[m][:, :], [(wd_hi[:, f, ms], wd_lo[:, f, ms], act_part(0, n, f), act_part(1, n, f))],
                             first=f == 0, last=f == FT - 1)
                mm.then_inc(down_done, 1)

            def expert_in(c):
                for e in range(E):
                    k = e // 4
                    i = E // 2 * c + e // 2
                    if e % 4 == 0:
                        pe.wait_ge(x3_hi_done, K * (c // 2) + k + 1)
                        pe.wait_ge(x3_lo_done, K * (c // 2) + k + 1)
                        pe.wait_ge(weight_lo, W_1 + k)
                    if e % 2 == 0 and i >= 3:
                        pe.wait_ge(gelu_done, 2 * (i - 2))
                    if e % 2 == 0 and i % 3:
                        pe.wait_ge(x3_done, K * (c // 2 + 1))
                    if i == 0:
                        pe.wait_ge(ln2_done, 1)
                    mm = mm3(expert_in_ps[i % 3][:, e % 2 * QT:(e % 2 + 1) * QT],
                             [(w1_hi[:, e], w1_lo[:, e], x3_hi[:, k, quarter(c)], x3_lo[:, k, quarter(c)])])
                    if e % 2:
                        mm.then_inc(e1_done, 1)

            def expert_out(c):
                pe.wait_ge(ld["w2"], 16)
                if c:
                    pe.wait_ge(y_done, K * c)
                else:
                    pe.wait_ge(ln2_done, 2)
                for g in range(2):
                    pe.wait_ge(gelu_done, E * c + 4 * g + 4)
                    for r in range(4):
                        mm = MM(expert_out_ps[32 * r:32 * r + 32, g * QT:(g + 1) * QT], w2_sb[:, 4 * g + r],
                                hid[4 * g + r][:, c % 2], start=True, stop=True)
                mm.then_inc(e2_done, 1)

            def row(a, c):
                return a[:, c % 2 * QT:(c % 2 + 1) * QT]

            def mean(c):
                pe.wait_ge(ysum_done, c + 1)
                if c:
                    pe.wait_ge(dev_done, c)
                else:
                    pe.wait_ge(x2_done, 2 * K)
                MM(mean_ps[:, 0:QT], avg[:], row(sqsum, c), start=True, stop=True).then_inc(mean_done, 1)

            def variance(c):
                pe.wait_ge(sqdsum_done, c + 1)
                if c:
                    pe.wait_ge(lnv_done, c)
                else:
                    pe.wait_ge(gate_done, 2 * FT)
                MM(var_ps[:, 0:QT], avg[:], row(sqsum, c), start=True, stop=True).then_inc(var_done, 1)

            def last_product(c):
                pe.wait_ge(s_hi_done, c + 1)
                pe.wait_ge(s_lo_done, c + 1)
                pe.wait_ge(weight_lo, W_OUT)
                if c:
                    pe.wait_ge(fin_done, K * c)
                else:
                    pe.wait_ge(shift_done, 2 * K)
                for m in range(K):
                    ms = slice(m * P, (m + 1) * P)
                    mm = mm3(last_ps[:, m * QT:(m + 1) * QT],
                             [(outw_hi[:, k, ms], outw_lo[:, k, ms], h4_hi[:, c % 2, k], h4_lo[:, c % 2, k])
                              for k in range(K)])
                mm.then_inc(out_mm, 1)

            def embedding():
                pe.wait_ge(scond_done, 1)
                pe.wait_ge(ld["embw"], 16)
                pe.wait_ge(ctxn_done, B)
                for m in range(2 * K):
                    for k in range(K):
                        mm = MM(last_ps[:, m * B:(m + 1) * B], emb_sb[:, k, m * P:(m + 1) * P], scond[:, k],
                                start=k == 0, stop=k == K - 1)
                mm.then_inc(emb_done, 1)

            scale_of(tw1_sb, bank[7], ld["tw1"], scale1_done)
            project(0)
            scale_of(tw2_sb, bank[6], ld["tw2"], scale2_done)
            project(1)
            turn_queries(0)
            turn_key(0)
            scores_for_max(0)
            for b in range(B):
                if b + 2 < B and b != 5:
                    project(b + 2)
                if b + 1 < B:
                    turn_queries(b + 1)
                    turn_key(b + 1)
                if b == 5:
                    pe.wait_ge(x2_done, 1)
                    project(b + 2)
                scores_transposed(b)
                if b + 1 < B:
                    scores_for_max(b + 1)
                weigh_values(b)
                if b == 4:
                    attn_out(0, 0)
                if b == 5:
                    attn_out(0, 1)
                if b == 6:
                    mean_of_squares(0)
            for f in range(FT):
                gate_or_up(0, f, 0)
                gate_or_up(0, f, 1)
                if f == 1:
                    attn_out(1, 0)
                    attn_out(1, 1)
                if f == 4:
                    mean_of_squares(1)
                if f == 5:
                    embedding()
            for f in range(FT):
                gate_or_up(1, f, 0)
                gate_or_up(1, f, 1)
                if f == 5:
                    down(0, 0)
                    down(0, 1)
            expert_in(0)
            expert_out(0)
            expert_in(1)
            mean(0)
            expert_out(1)
            down(1, 0)
            variance(0)
            mean(1)
            down(1, 1)
            variance(1)
            last_product(0)
            last_product(1)
            expert_in(2)
            expert_out(2)
            expert_in(3)
            mean(2)
            expert_out(3)
            variance(2)
            mean(3)
            variance(3)
            last_product(2)
            last_product(3)


def kernel(x, pos_BxS, cond_2048, L0_cond_ln1_w, L0_cond_ln1_tw, L0_cond_ln2_w, L0_cond_ln2_tw, L0_cond_Wq,
           L0_cond_Wk, L0_cond_Wv, L0_cond_Wo, L0_cond_Wg, L0_cond_Wu, L0_cond_Wd, L1_cond_W1, L1_cond_b1,
           L1_cond_W2, L1_cond_b2, L1_cond_emb_W, L1_cond_emb_b, L1_cond_ln_g, L1_cond_ln_b, L1_cond_out_W,
           L1_cond_out_b):
    import numpy as np
    import concourse.bacc as bacc
    from concourse.bass_utils import run_bass_kernel_spmd

    def tiles(a, axis=0):
        a = np.asarray(a)
        return a.reshape(a.shape[0] // P, P, -1).transpose(1, 0, 2)

    def turned(w):
        return tiles(np.asarray(w).T)

    x = np.asarray(x)
    inv_freq = (np.float32(1.0) / np.float32(10000.0) ** (np.arange(0, HD, 2, dtype=np.float32) / np.float32(HD)))
    small = np.concatenate(
        [np.asarray(a).reshape(-1, P).T for a in (L0_cond_ln1_w, L0_cond_ln2_w, L1_cond_ln_g, L1_cond_ln_b,
                                                  L1_cond_out_b, L1_cond_b2, L1_cond_emb_b, L1_cond_b1)]
        + [tiles(np.asarray(cond_2048).T).reshape(P, K * B), np.tile(inv_freq.astype(np.float32), (P, 1))], axis=1)
    wg, wu = (np.asarray(w).reshape(FT, P, K, P) for w in (L0_cond_Wg, L0_cond_Wu))
    arrays = {
        "xT": tiles(x.reshape(T, H).T),
        "xn": x.transpose(1, 0, 2),
        "small": small,
        "posT": np.asarray(pos_BxS).T,
        "ident": np.eye(P, dtype=np.float32),
        "tw1": turned(L0_cond_ln1_tw),
        "tw2": turned(L0_cond_ln2_tw),
        "wqkv": turned(np.concatenate([np.asarray(w) for w in (L0_cond_Wq, L0_cond_Wk, L0_cond_Wv)])),
        "wo": turned(L0_cond_Wo),
        "wgu": np.stack([wg, wu], axis=1).transpose(4, 0, 1, 3, 2),
        "wd": turned(L0_cond_Wd),
        "w1": np.asarray(L1_cond_W1).transpose(1, 0, 2),
        "w2": np.asarray(L1_cond_W2).transpose(1, 0, 2),
        "embw": tiles(L1_cond_emb_W),
        "outw": tiles(L1_cond_out_W),
    }
    nc = bacc.Bacc("TRN2", target_bir_lowering=False, num_devices=1)
    feed, args = {}, []
    for name, a in arrays.items():
        a = np.ascontiguousarray(a)
        feed[f"in_{name}"] = a
        args.append(nc.dram_tensor(f"in_{name}", a.shape, mybir.dt.from_np(a.dtype), kind="ExternalInput").ap())
    args.append(nc.dram_tensor("out_yT", (P, K, T), F32, kind="ExternalOutput").ap())
    cond_block_kernel(nc, *args)
    r = run_bass_kernel_spmd(nc, [feed], core_ids=[0])
    yT = r.results[0]["out_yT"]
    return yT.transpose(1, 0, 2).reshape(H, T).T.reshape(B, S, H)
```

```python
from contextlib import ExitStack

import concourse.bass as bass
from concourse import mybir

F32 = mybir.dt.float32
F32R = mybir.dt.float32r
BF16 = mybir.dt.bfloat16
I32 = mybir.dt.int32
ALU = mybir.AluOpType
ACT = mybir.ActivationFunctionType
AX = mybir.AxisListType

P = 128
B, S, H = 8, 128, 256
T = B * S
K = H // P
NH, HD = 8, 32
QK = (NH + 1) * HD
QKV = QK + HD
FR = HD // 2
INTER = 1024
FT = INTER // P
E, LAT, FFN = 8, 32, 128
NB = 4
HT = NB * S
QT = HT // 2
QS = QT // S
QUARTERS = T // QT
CHUNKS = ((0, HT), (HT, QT), (HT + QT, QT))
CHUNK_OF_QUARTER = (0, 0, 1, 2)
HG = 4
RMS_EPS, LN_EPS = 1e-6, 1e-5
PI = 3.14159265358979
MAGIC = 1.5 * 2.0 ** 23
TAU_A = 6.28125
TAU_B = 1.934051513671875e-3
TAU_C = 2 * PI - TAU_A - TAU_B

POOL_LOWS = FT - 2
RAW_TILES = 4
NORM_GROUPS = tuple((b, b + 2) for b in range(0, B, 2))

TABLE_READY = 10

C_LN1W, C_LN2W, C_LNG, C_LNB, C_OUTB, C_B2, C_EMBB, C_B1, C_COND, C_INVF, C_END = (
    0, 2, 4, 6, 8, 10, 12, 16, 24, 40, 56)


def cond_block_kernel(nc, xT, xn, small, posT, ident, tw1, tw2, wqkv, wo, wgu, wd, w1, w2, embw, outw, out):
    ctx = ExitStack()
    with ctx:
        def sb(name, shape, dt=F32):
            return ctx.enter_context(nc.sbuf_tensor(name, shape, dt))

        def sem(name):
            return ctx.enter_context(nc.semaphore(name))

        res_sb = sb("res_sb", [P, K, T])
        xn_sb = sb("xn_sb", [P, B, H])
        small_sb = sb("small_sb", [P, C_END])
        pos_sb = sb("pos_sb", [P, B], I32)
        id_sb = sb("id_sb", [P, P])
        tw_sb = sb("tw_sb", [P, 2, K, H])
        tw1_sb, tw2_sb = tw_sb[:, 0], tw_sb[:, 1]
        emb_sb = sb("emb_sb", [P, K, 2 * H])
        w2_sb = sb("w2_sb", [P, E, LAT])
        sq_raw = sb("sq_raw", [P, K, H])
        wgu_raw = sb("wgu_raw", [P, RAW_TILES, 2, K, P])
        wd_raw = sb("wd_raw", [P, FT, H])
        w1_raw = tw_sb[:].rearrange("p n k h -> p (n k h)").rearrange("p (e f) -> p e f", e=E)
        early = sb("early", [P, 2 * E * FFN], F32R)
        wqkv_hi = early[:, 0:K * QKV].rearrange("p (k m) -> p k m", k=K)
        wqkv_lo = early[:, K * QKV:2 * K * QKV].rearrange("p (k m) -> p k m", k=K)
        xg_lo = early[:, 2 * K * QKV:2 * K * QKV + 3 * K * S].rearrange("p (r k s) -> p r k s", r=3, k=K)
        wo_hi, wo_lo = sb("wo_hi", [P, K, H], F32R), sb("wo_lo", [P, K, H], F32R)
        wgu_hi, wgu_lo = sb("wgu_hi", [P, FT, 2, K, P], F32R), sb("wgu_lo", [P, FT, 2, K, P], F32R)
        wd_hi, wd_lo = sb("wd_hi", [P, FT, H], F32R), sb("wd_lo", [P, FT, H], F32R)
        w1_hi, w1_lo = (early[:, c * E * FFN:(c + 1) * E * FFN].rearrange("p (e f) -> p e f", e=E) for c in range(2))
        outw_hi, outw_lo = sb("outw_hi", [P, K, H], F32R), sb("outw_lo", [P, K, H], F32R)
        negid = sb("negid", [P, P], BF16)
        avg = sb("avg", [P, P])
        ones = sb("ones", [P, HD])
        filler = sb("filler", [P, P], BF16)
        gain1 = sb("gain1", [P, K, B])
        gain2 = sb("gain2", [P, K, B])
        scond = sb("scond", [P, K, B])
        eps_sb = sb("eps_sb", [P, 2])
        shiftb = sb("shiftb", [P, 2 * K, B])
        lnA = sb("lnA", [P, K, B])
        lnB = sb("lnB", [P, K, B])
        posf = sb("posf", [P, B])
        ang = sb("ang", [P, B * FR])
        prob = sb("prob", [P, 2, NH, S])
        first = prob[:].rearrange("p a h s -> p (a h s)")
        turn, whole, *red = (first[:, c * 2 * B * FR:(c + 1) * 2 * B * FR].rearrange("p (c n) -> p c n", c=2)
                             for c in range(5))
        wqkv_raw = first[:, 10 * B * FR:10 * B * FR + K * QKV].rearrange("p (k m) -> p k m", k=K)
        trig = sb("trig", [P, 2, B, FR])
        cs = sb("cs", [P, 2, B, FR])
        ms1 = sb("ms1", [P, B])
        ln1 = sb("ln1", [P, B])
        rstd1 = sb("rstd1", [P, B])
        xg_hi = sb("xg_hi", [P, 3, K, S], F32R)
        ropeA, ropeB = sb("ropeA", [P, QK]), sb("ropeB", [P, QK])
        qk = sb("qk", [P, 2, NH + 1, HD])
        stack = sb("stack", [P, 2, NH + 1, 3, HD])
        qkT = sb("qkT", [P, 2, NH, S], F32R)
        kT = sb("kT", [P, 2, S], F32R)
        v_sb = sb("v_sb", [P, B, HD])
        top = sb("top", [P, 2, NH], BF16)
        rden = sb("rden", [P, K, S])
        ctxn = sb("ctxn", [P, 2, K, S])
        ctx_hi, ctx_lo = sb("ctx_hi", [P, K, HT], F32R), sb("ctx_lo", [P, K, HT], F32R)
        lnrow = sb("lnrow", [P, HT])
        rstd = sb("rstd", [P, HT])
        sqsum = sb("sqsum", [P, HT])
        h_hi, h_lo = sb("h_hi", [P, K, HT], F32R), sb("h_lo", [P, K, HT], F32R)
        act = sb("act", [P, 2, HT])
        act_hi, act_lo = sb("act_hi", [P, FT, HT], F32R), sb("act_lo", [P, FT, HT], F32R)
        hf = xn_sb[:, 0:NB, :].rearrange("p b h -> p (b h)").rearrange("p (k t) -> p k t", k=K)
        sq = xn_sb[:, NB:B, :].rearrange("p b h -> p (b h)").rearrange("p (k t) -> p k t", k=K)
        s4, sq4 = (a.rearrange("p k t -> p (k t)").rearrange("p (c k t) -> p c k t", c=2, k=K) for a in (hf, sq))
        s4_hi, s4_lo = (qkT[:, i].rearrange("p h s -> p (h s)").rearrange("p (c k t) -> p c k t", c=2, k=K)
                        for i in range(2))
        hid = [four[:, e] for four in (
            wgu_raw[:].rearrange("p f g k m -> p (f g k m)").rearrange("p (e c t) -> p e c t", e=HG, c=2),
            first.rearrange("p (e c t) -> p e c t", e=HG, c=2)) for e in range(HG)]
        yln = wd_raw[:].rearrange("p f h -> p (f h)").rearrange("p (c i k t) -> p c i k t", c=2, i=2, k=K)
        x3_hi, x3_lo = ctx_hi, ctx_lo

        bank = [ctx.enter_context(nc.psum_tensor(f"bank{i}", [P, 512], F32)) for i in range(8)]
        proj_ps, ctx_ps = bank[0], bank[1]
        score_ps = bank[4:6]

        def pair(b):
            return bank[6:8] if b % 2 else bank[2:4]

        GATE_UP_BANK = ((2,) * FT, (2, 3, 0, 2, 3, 0, 2, 3), (4, 2, 3, 1, 0, 2, 3, 0))

        def gate_up_ps(n, f):
            b = GATE_UP_BANK[n][f]
            return (bank[b], bank[b + 1]) if n == 0 else (bank[b][:, 0:QT], bank[b][:, QT:2 * QT])

        def last_in_bank(n, f):
            banks = [{b, b + 1} if a == 0 else {b} for a in range(len(CHUNKS)) for b in GATE_UP_BANK[a]]
            i = FT * n + f
            return max((j + 1 for j in range(i) if banks[j] & banks[i]), default=0)

        down_ps = bank[6:8]
        attn_out_ps = ((bank[1], bank[0]), (bank[4], bank[5]))
        ms2_ps = (bank[0], bank[4])
        expert_in_ps = (bank[0], bank[6], bank[7], bank[5])
        expert_out_ps, mean_ps = bank[4], bank[5]
        emb_ps = bank[0]
        var_ps = (bank[1], bank[1], bank[4], bank[3])

        def last_ps(c, m):
            return (bank[2], bank[4])[m][:, 0:QT] if c == QUARTERS - 1 else bank[1][:, m * QT:(m + 1) * QT]

        ld = {n: sem("ld_" + n) for n in (
            "small", "ident", "pos", "tw1", "tw2", "xT_first", "xT0", "xT1", "xn0", "xn1", "xn_rest", "wqkv", "wo",
            "wgu0", "wgu1", "wgu2", "wgu3", "wd", "w1", "w2", "embw", "outw")}
        eps_ready, filler_ready = sem("eps_ready"), sem("filler_ready")
        zeroed, consts_ready, negid_ready = sem("zeroed"), sem("consts_ready"), sem("negid_ready")
        wqkv_split, weight_hi, weight_lo = sem("wqkv_split"), sem("weight_hi"), sem("weight_lo")
        scale1_done, gain1_done = sem("scale1_done"), sem("gain1_done")
        scale2_done, gain2_done = sem("scale2_done"), sem("gain2_done")
        scond_done, emb_done, shift_done, lnab_done = (
            sem("scond_done"), sem("emb_done"), sem("shift_done"), sem("lnab_done"))
        table_step, trig_done, ms1_done, ln1_done, rstd1_done, cs_done = (
            sem("table_step"), sem("trig_done"), sem("ms1_done"), sem("ln1_done"), sem("rstd1_done"), sem("cs_done"))
        xg_hi_done, xg_lo_done, proj_done = sem("xg_hi_done"), sem("xg_lo_done"), sem("proj_done")
        rope_mul, rope_done, v_done = sem("rope_mul"), sem("rope_done"), sem("v_done")
        qk_hi_done, qk_lo_done = sem("qk_hi_done"), sem("qk_lo_done")
        turned, kturned, qT_done, kT_done = sem("turned"), sem("kturned"), sem("qT_done"), sem("kT_done")
        s1_done, top_done, st_done, exp_done = sem("s1_done"), sem("top_done"), sem("st_done"), sem("exp_done")
        pv_done, lden_done, rden_done, ctxn_done = (
            sem("pv_done"), sem("lden_done"), sem("rden_done"), sem("ctxn_done"))
        ctx_hi_done, ctx_lo_done = sem("ctx_hi_done"), sem("ctx_lo_done")
        wo_done, x2_done = sem("wo_done"), sem("x2_done")
        sq2_done, sqsum2_done, ms2_done, ln2_done, rstd2_done = (
            sem("sq2_done"), sem("sqsum2_done"), sem("ms2_done"), sem("ln2_done"), sem("rstd2_done"))
        h_done, h_hi_done, h_lo_done = sem("h_done"), sem("h_hi_done"), sem("h_lo_done")
        gate_mm, up_mm, gate_done, act_done = sem("gate_mm"), sem("up_mm"), sem("gate_done"), sem("act_done")
        act_hi_done, act_lo_done = sem("act_hi_done"), sem("act_lo_done")
        down_done, x3_done, x3_hi_done, x3_lo_done = (
            sem("down_done"), sem("x3_done"), sem("x3_hi_done"), sem("x3_lo_done"))
        e1_done, gelu_done, e2_done, y_done = sem("e1_done"), sem("gelu_done"), sem("e2_done"), sem("y_done")
        ysum_done, mean_done, dev_done, sqd_done, sqdsum_done, var_done, lnv_done, rstdv_done = (
            sem("ysum_done"), sem("mean_done"), sem("dev_done"), sem("sqd_done"), sem("sqdsum_done"),
            sem("var_done"), sem("lnv_done"), sem("rstdv_done"))
        z_done, s_done, s_hi_done, s_lo_done = sem("z_done"), sem("s_done"), sem("s_hi_done"), sem("s_lo_done")
        out_mm, fin_done, stored = sem("out_mm"), sem("fin_done"), sem("stored")

        W_WO, W_GU, W_D, W_1, W_OUT = 1, 2, 2 + FT, 2 + 2 * FT, 4 + 2 * FT
        block = ctx.enter_context(nc.Block())

        def half(n):
            return slice(n * HT, (n + 1) * HT)

        def quarter(c):
            return slice(c * QT, (c + 1) * QT)

        def quarter_in_half(c):
            return quarter(c % 2)

        def chunk(n):
            return slice(CHUNKS[n][0], sum(CHUNKS[n]))

        def chunk_in_half(n):
            return slice(CHUNKS[n][0] % HT, CHUNKS[n][0] % HT + CHUNKS[n][1])

        def width(n):
            return CHUNKS[n][1]

        def tok(b):
            return slice(b % NB * S, (b % NB + 1) * S)

        @block.sync
        def _(sp):
            sp.dma_start(small_sb[:], small).then_inc(ld["small"], 16)
            sp.dma_start(pos_sb[:], posT).then_inc(ld["pos"], 16)
            sp.dma_start(tw1_sb[:], tw1).then_inc(ld["tw1"], 16)
            sp.dma_start(xn_sb[:, 0:2], xn[:, 0:2]).then_inc(ld["xn0"], 16)
            sp.dma_start(wqkv_raw, wqkv).then_inc(ld["wqkv"], 16)
            sp.dma_start(res_sb[:, :, 0:S], xT[:, :, 0:S]).then_inc(ld["xT_first"], 16)
            sp.dma_start(res_sb[:, :, S:HT], xT[:, :, S:HT]).then_inc(ld["xT0"], 16)
            sp.dma_start(xn_sb[:, 2:NB], xn[:, 2:NB]).then_inc(ld["xn1"], 16)
            sp.dma_start(id_sb[:], ident).then_inc(ld["ident"], 16)
            sp.dma_start(xn_sb[:, NB:B], xn[:, NB:B]).then_inc(ld["xn_rest"], 16)
            sp.dma_start(tw2_sb[:], tw2).then_inc(ld["tw2"], 16)
            sp.dma_start(sq_raw[:], wo).then_inc(ld["wo"], 16)
            sp.dma_start(res_sb[:, :, half(1)], xT[:, :, half(1)]).then_inc(ld["xT1"], 16)
            sp.dma_start(emb_sb[:], embw).then_inc(ld["embw"], 16)
            for c in range(4):
                if c == 2:
                    sp.dma_start(wd_raw[:], wd).then_inc(ld["wd"], 16)
                if c >= 2:
                    sp.wait_ge(weight_lo, W_GU + 2 * c - 3)
                r = 2 * c % RAW_TILES
                sp.dma_start(wgu_raw[:, r:r + 2], wgu[:, 2 * c:2 * c + 2]).then_inc(ld[f"wgu{c}"], 16)
            sp.wait_ge(zeroed, 1)
            for r in range(4):
                sp.dma_start(w1_raw[32 * r:32 * r + 32, r::4], w1[:, r::4]).then_inc(ld["w1"], 16)
            sp.dma_start(w2_sb[:], w2).then_inc(ld["w2"], 16)
            sp.dma_start(sq_raw[:], outw).then_inc(ld["outw"], 16)
            for c in range(QUARTERS - 1):
                sp.wait_ge(fin_done, K * (c + 1))
                sp.dma_start(out[:, :, quarter(c)], res_sb[:, :, quarter(c)]).then_inc(stored, 16)
            for m in range(K):
                sp.wait_ge(fin_done, K * (QUARTERS - 1) + m + 1)
                sp.dma_start(out[:, m, quarter(c + 1)], res_sb[:, m, quarter(c + 1)]).then_inc(stored, 16)
            sp.wait_ge(stored, 16 * (QUARTERS - 1 + K))

        @block.gpsimd
        def _(pool):
            nc.gpsimd.memset(filler[:], 1.0).then_inc(filler_ready, 1)
            nc.gpsimd.memset(avg[:], 1.0 / H).then_inc(consts_ready, 1)
            nc.gpsimd.memset(ones[:], 1.0).then_inc(consts_ready, 1)

            def split(raw, hi, lo, loads):
                for s, n in loads:
                    pool.wait_ge(s, n)
                nc.gpsimd.tensor_copy(hi, raw).then_inc(weight_hi, 1)
                split.n += 1
                pool.wait_ge(weight_hi, split.n)
                nc.gpsimd.tensor_tensor(lo, raw, hi.bitcast(F32), ALU.subtract).then_inc(weight_lo, 1)
            split.n = 0
            split(sq_raw[:], wo_hi[:], wo_lo[:], [(ld["wo"], 16)])
            pool.wait_ge(scale1_done, 1)
            pool.wait_ge(scale2_done, 1)
            nc.gpsimd.memset(w1_raw, 0.0).then_inc(zeroed, 1)
            for f in range(FT):
                split(wgu_raw[:, f % RAW_TILES], wgu_hi[:, f], wgu_lo[:, f], [(ld[f"wgu{f // 2}"], 16)])

            def act_low(n, f):
                if f == 0 and n:
                    pool.wait_ge(act_lo_done, FT * n)
                pool.wait_ge(act_hi_done, FT * n + f + 1)
                nc.gpsimd.tensor_tensor(act_lo[:, f, chunk_in_half(n)], act[:, f % 2, 0:width(n)],
                                        act_hi[:, f, chunk_in_half(n)].bitcast(F32),
                                        ALU.subtract).then_inc(act_lo_done, 1)
            for f in range(FT):
                split(wd_raw[:, f], wd_hi[:, f], wd_lo[:, f], [(ld["wd"], 16)])
            pool.wait_ge(proj_done, B)
            for c in range(2):
                four = slice(4 * c, 4 * c + 4)
                split(w1_raw[:, four], w1_hi[:, four], w1_lo[:, four], [(ld["w1"], 64)])
            split(sq_raw[:], outw_hi[:], outw_lo[:], [(ld["outw"], 16)])
            for n in range(len(CHUNKS)):
                for f in range(POOL_LOWS):
                    act_low(n, f)

        @block.scalar
        def _(act_e):
            A = nc.scalar.activation

            def mean_square(sequences):
                for b in sequences:
                    act_e.wait_ge(ld[f"xn{b // 2}" if b < NB else "xn_rest"], 16)
                    if b >= NB:
                        act_e.wait_ge(ms1_done, b - NB + 1)
                    A(sq_junk(b), xn_sb[:, b], ACT.Square, accum_out=ms1[:, b:b + 1]).then_inc(ms1_done, 1)

            def sq_junk(b):
                return act[:].rearrange("p a t -> p (a t)")[:, b % NB * H:(b % NB + 1) * H]

            def rstd_first(g):
                bs = slice(*NORM_GROUPS[g])
                act_e.wait_ge(ms1_done, bs.stop)
                A(ln1[:, bs], ms1[:, bs], ACT.Ln, scale=1.0 / H, bias=eps_rms).then_inc(ln1_done, 1)
                act_e.wait_ge(ln1_done, g + 1)
                A(rstd1[:, bs], ln1[:, bs], ACT.Exp, scale=-0.5).then_inc(rstd1_done, 1)

            eps_rms, eps_ln = eps_sb[:, 0:1], eps_sb[:, 1:2]

            def xg_high(b):
                act_e.wait_ge(ld[f"xT{b // NB}" if b else "xT_first"], 16)
                act_e.wait_ge(gain1_done, K)
                if b >= 3:
                    act_e.wait_ge(proj_done, b - 2)
                for k in range(K):
                    A(xg_hi[:, b % 3, k], res_sb[:, k, b * S:(b + 1) * S], ACT.Copy,
                      scale=gain1[:, k, b:b + 1]).then_inc(xg_hi_done, 1)

            def stack_high(b):
                act_e.wait_ge(rope_done, 2 * (b + 1))
                if b >= 2:
                    act_e.wait_ge(turned, 2 * (b - 1))
                    act_e.wait_ge(kturned, b - 1)
                st = stack[:, b % 2].bitcast(F32R)
                A(st[:, 0:NH, 0::2],
                  qk[:, b % 2, 0:NH].rearrange("p h (c d) -> p h c d", c=1).broadcast_to([P, NH, 2, HD]),
                  ACT.Copy).then_inc(qk_hi_done, 1)
                A(st[:, NH, 0:2], qk[:, b % 2, NH:NH + 1].broadcast_to([P, 2, HD]), ACT.Copy).then_inc(qk_hi_done, 1)

            def take_turned(b):
                if b >= 2:
                    act_e.wait_ge(st_done, 2 * (b - 1))
                act_e.wait_ge(kturned, b + 1)
                A(kT[0:96, b % 2], score_ps[0][0:96, 0:S], ACT.Copy).then_inc(kT_done, 1)
                for g in range(2):
                    act_e.wait_ge(turned, 2 * b + g + 1)
                    A(qkT[0:96, b % 2, HG * g:HG * g + HG].rearrange("p h s -> p (h s)"), pair(b)[g][0:96, :],
                      ACT.Copy).then_inc(qT_done, 1)

            def exps(b):
                if b >= 2:
                    act_e.wait_ge(pv_done, b - 1)
                for g in range(2):
                    act_e.wait_ge(st_done, 2 * b + g + 1)
                    A(prob[:, b % 2, HG * g:HG * g + HG].rearrange("p h s -> p (h s)"), pair(b)[g][:, :], ACT.Exp,
                      scale=HD ** -0.5).then_inc(exp_done, 1)

            def reciprocal_of_sum(b):
                act_e.wait_ge(pv_done, b + 1)
                if b >= 1:
                    act_e.wait_ge(ctxn_done, b)
                A(rden[:], ctx_ps[:, K * S:2 * K * S].rearrange("p (k s) -> p k s", k=K), ACT.Ln).then_inc(lden_done, 1)
                act_e.wait_ge(lden_done, b + 1)
                A(rden[:], rden[:], ACT.Exp, scale=-1.0).then_inc(rden_done, 1)

            def ctx_high(b):
                act_e.wait_ge(ctxn_done, b + 1)
                if b == NB:
                    act_e.wait_ge(wo_done, K)
                A(ctx_hi[:, :, tok(b)], ctxn[:, b % 2], ACT.Copy).then_inc(ctx_hi_done, 1)

            def x2_squares(n):
                for k in range(K):
                    act_e.wait_ge(x2_done, K * n + k + 1)
                    if n:
                        act_e.wait_ge(sqsum2_done, n)
                    A(sq[:, k], res_sb[:, k, half(n)], ACT.Square).then_inc(sq2_done, 1)

            def rstd_second(n):
                act_e.wait_ge(ms2_done, n + 1)
                if n:
                    act_e.wait_ge(h_done, NB * K * n)
                A(lnrow[:], ms2_ps[n][:, :], ACT.Ln, bias=eps_rms).then_inc(ln2_done, 1)
                act_e.wait_ge(ln2_done, n + 1)
                A(rstd[:], lnrow[:], ACT.Exp, scale=-0.5).then_inc(rstd2_done, 1)

            def h_high(n, tiles=range(K)):
                if n:
                    act_e.wait_ge(up_mm, FT * n)
                for k in tiles:
                    act_e.wait_ge(h_done, NB * (K * n + k + 1))
                    A(h_hi[:, k], hf[:, k], ACT.Copy).then_inc(h_hi_done, 1)

            def silu(n, f):
                i = FT * n + f
                act_e.wait_ge(up_mm if n else gate_mm, i + 1)
                if i >= 2:
                    act_e.wait_ge(act_hi_done, i - 1)
                    act_e.wait_ge(act_lo_done, i - 1)
                A(act[:, i % 2, 0:width(n)], gate_up_ps(n, f)[0][:, 0:width(n)], ACT.Silu).then_inc(gate_done, 1)

            def silu_then_high(n, f):
                if f + 1 < FT:
                    silu(n, f + 1)
                act_high(n, f)

            def act_high(n, f):
                i = FT * n + f
                act_e.wait_ge(act_done, i + 1)
                if n:
                    act_e.wait_ge(down_done, K)
                A(act_hi[:, f, chunk_in_half(n)], act[:, i % 2, 0:width(n)], ACT.Copy).then_inc(act_hi_done, 1)

            def x3_high(n, tiles=range(K)):
                for m in tiles:
                    act_e.wait_ge(x3_done, K * n + m + 1)
                    if n:
                        act_e.wait_ge(e1_done, E // 2 * n)
                    A(x3_hi[:, m, chunk_in_half(n)], res_sb[:, m, chunk(n)], ACT.Copy).then_inc(x3_hi_done, 1)

            def gelu(c):
                for e in range(E):
                    act_e.wait_ge(e1_done, E // 2 * c + e // 2 + 1)
                    if c >= 2:
                        act_e.wait_ge(e2_done, c - 1)
                    A(hid[e][:, c % 2], expert_in_ps[e // 2][:, e % 2 * QT:(e % 2 + 1) * QT], ACT.Gelu,
                      bias=small_sb[:, C_B1 + e:C_B1 + e + 1]).then_inc(gelu_done, 1)

            def norm_squares(c):
                if c >= 2:
                    act_e.wait_ge(sqdsum_done, c - 1)
                for k in range(K):
                    act_e.wait_ge(dev_done, K * c + k + 1)
                    A(sq4[:, c % 2, k], yln[:, c % 2, 1, k], ACT.Square).then_inc(sqd_done, 1)

            def row(a, c):
                return a[:, c % 2 * QT:(c % 2 + 1) * QT]

            def norm_rstd(c):
                act_e.wait_ge(var_done, max(c + 1, 2))
                if c >= 2:
                    act_e.wait_ge(z_done, c - 1)
                A(row(lnrow, c), row(var_ps[c], c), ACT.Ln, bias=eps_ln).then_inc(lnv_done, 1)
                act_e.wait_ge(lnv_done, c + 1)
                A(row(rstd, c), row(lnrow, c), ACT.Exp, scale=-0.5).then_inc(rstdv_done, 1)

            def norm_silu(c, tiles=range(K)):
                act_e.wait_ge(lnab_done, 3)
                act_e.wait_ge(z_done, c + 1)
                if c >= 2:
                    act_e.wait_ge(s_lo_done, K * (c - 1))
                    act_e.wait_ge(out_mm, K * (c - 1))
                for k in tiles:
                    for j in range(QS):
                        b = QS * c + j
                        A(s4[:, c % 2, k, j * S:(j + 1) * S], yln[:, c % 2, 0, k, j * S:(j + 1) * S], ACT.Silu,
                          scale=lnA[:, k, b:b + 1], bias=lnB[:, k, b:b + 1]).then_inc(s_done, 1)
                    act_e.wait_ge(s_done, QS * (K * c + k + 1))
                    A(s4_hi[:, c % 2, k], s4[:, c % 2, k], ACT.Copy).then_inc(s_hi_done, 1)

            def table(name):
                nc.scalar.preload_act_table_set(name)

            table("silu_and_others")
            act_e.wait_ge(ld["small"], 16)
            A(scond[:].rearrange("p k b -> p (k b)"), small_sb[:, C_COND:C_COND + K * B],
              ACT.Silu).then_inc(scond_done, 1)
            table("trig_and_small")
            mean_square([0, 1])
            act_e.wait_ge(ld["wqkv"], 16)
            A(wqkv_hi, wqkv_raw, ACT.Copy).then_inc(wqkv_split, 1)
            act_e.wait_ge(table_step, TABLE_READY)
            A(trig[:].rearrange("p c b f -> p (c b f)"), red[2].rearrange("p c n -> p (c n)"),
              ACT.Sin).then_inc(trig_done, 1)
            xg_high(0)
            table("natural_log_exp_and_others")
            act_e.wait_ge(eps_ready, 2)
            rstd_first(0)
            mean_square([2, 3])
            rstd_first(1)
            stack_high(0)
            xg_high(2)
            mean_square([4, 5])
            rstd_first(2)
            take_turned(0)
            stack_high(1)
            for b in range(B):
                if b == NB + 3:
                    h_high(0, [0])
                if b >= 1:
                    reciprocal_of_sum(b - 1)
                if b == NB + 3:
                    exps(b)
                    h_high(0, [1])
                if b == 0:
                    xg_high(3)
                if b == NB:
                    ctx_high(b - 1)
                if b + 1 < B:
                    take_turned(b + 1)
                if b == NB + 2:
                    rstd_second(0)
                if b < NB + 3:
                    exps(b)
                if b >= 1 and b != NB:
                    ctx_high(b - 1)
                if b + 2 < B:
                    stack_high(b + 2)
                if b + 4 < B:
                    xg_high(b + 4)
                if b in (1, 2):
                    mean_square([b + 5])
                if b == 3:
                    rstd_first(3)
                if b == NB + 1:
                    x2_squares(0)
            reciprocal_of_sum(B - 1)
            table("silu_and_others")
            silu(0, 0)
            ctx_high(B - 1)
            for f in range(FT):
                silu_then_high(0, f)
                if f == 3:
                    x2_squares(1)
            table("natural_log_exp_and_others")
            rstd_second(1)
            h_high(1)
            table("gelu_and_others")
            x3_high(0)
            gelu(0)
            gelu(1)
            table("silu_and_others")
            silu(1, 0)
            for f in range(FT):
                silu_then_high(1, f)
                if f in (3, 4):
                    norm_squares(f - 3)
            table("natural_log_exp_and_others")
            norm_rstd(0)
            norm_rstd(1)
            table("silu_and_others")
            x3_high(1, [0])
            silu(2, 0)
            x3_high(1, [1])
            norm_silu(0)
            silu_then_high(2, 0)
            act_high(2, 1)
            table("gelu_and_others")
            gelu(2)
            table("silu_and_others")
            silu(2, 2)
            for f in range(2, FT):
                silu_then_high(2, f)
                if f in (2, 3):
                    norm_silu(1, [f - 2])
                if f == 5:
                    norm_squares(2)
            table("natural_log_exp_and_others")
            x3_high(2, [0])
            norm_rstd(2)
            table("gelu_and_others")
            x3_high(2, [1])
            gelu(3)
            table("silu_and_others")
            norm_silu(2)
            table("natural_log_exp_and_others")
            norm_rstd(3)
            table("silu_and_others")
            norm_silu(3)

        @block.vector
        def _(dve):
            TT, TS, STT = nc.vector.tensor_tensor, nc.vector.tensor_scalar, nc.vector.scalar_tensor_tensor

            def col(c, n=1):
                return small_sb[:, c:c + n]

            nc.vector.memset(eps_sb[:, 0:1], RMS_EPS).then_inc(eps_ready, 1)
            nc.vector.memset(eps_sb[:, 1:2], LN_EPS).then_inc(eps_ready, 1)

            def rotary_tables():
                dve.wait_ge(ld["pos"], 16)
                dve.wait_ge(ld["small"], 16)
                n = [0]

                def then(ins):
                    n[0] += 1
                    ins.then_inc(table_step, 1)
                    dve.wait_ge(table_step, n[0])
                both = [P, 2, B * FR]
                then(nc.vector.tensor_copy(posf[:], pos_sb[:]))
                then(TT(ang[:].rearrange("p (b f) -> p b f", b=B),
                        posf[:].rearrange("p (b f) -> p b f", f=1).broadcast_to([P, B, FR]),
                        col(C_INVF, FR).rearrange("p (b f) -> p b f", b=1).broadcast_to([P, B, FR]), ALU.mult))
                then(TS(turn[:, 0], ang[:], 0.5 / PI, 0.25, ALU.mult, ALU.add))
                then(TS(turn[:, 1], ang[:], 0.5 / PI, None, ALU.mult))
                then(TS(whole, turn, MAGIC, -MAGIC, ALU.add, ALU.add))
                then(STT(red[0], whole, -TAU_A, ang[:].rearrange("p (c n) -> p c n", c=1).broadcast_to(both),
                         ALU.mult, ALU.add))
                then(STT(red[1], whole, -TAU_B, red[0], ALU.mult, ALU.add))
                then(STT(red[0], whole, -TAU_C, red[1], ALU.mult, ALU.add))
                then(TS(red[0][:, 0], red[0][:, 0], PI / 2, None, ALU.add))
                TS(red[2], red[0], 3.1415925, -3.1415925, ALU.min, ALU.max).then_inc(table_step, 1)
                assert n[0] + 1 == TABLE_READY

            def scaled_table(g):
                dve.wait_ge(trig_done, 1)
                dve.wait_ge(rstd1_done, g + 1)
                bs = slice(*NORM_GROUPS[g])
                for c in range(2):
                    TT(cs[:, c, bs], trig[:, c, bs],
                       rstd1[:, bs].rearrange("p (b f) -> p b f", f=1).broadcast_to([P, bs.stop - bs.start, FR]),
                       ALU.mult).then_inc(cs_done, 1)

            def gains(ps, w_col, gain, mm_done, done):
                dve.wait_ge(mm_done, 1)
                for m in range(K):
                    TS(gain[:, m], ps[:, m * B:(m + 1) * B], 1.0, col(w_col + m), ALU.add, ALU.mult).then_inc(done, 1)

            def second_xg_high():
                dve.wait_ge(ld["xT0"], 16)
                dve.wait_ge(xg_hi_done, K)
                for k in range(K):
                    TS(xg_hi[:, 1, k], res_sb[:, k, S:2 * S], gain1[:, k, 1:2], None, ALU.mult).then_inc(xg_hi_done, 1)

            def xg_low(b):
                for k in range(K):
                    dve.wait_ge(xg_hi_done, K * b + k + 1)
                    if b >= 3 and k == 0:
                        dve.wait_ge(proj_done, b - 2)
                    STT(xg_lo[:, b % 3, k], res_sb[:, k, b * S:(b + 1) * S], gain1[:, k, b:b + 1],
                        xg_hi[:, b % 3, k].bitcast(F32), ALU.mult, ALU.subtract).then_inc(xg_lo_done, 1)

            def rope(b):
                dve.wait_ge(proj_done, b + 1)
                dve.wait_ge(cs_done, 2 * (b // 2 + 1))
                if b >= 1:
                    dve.wait_ge(rope_done, 2 * b)
                heads = [P, 2 * (NH + 1), FR]
                for c, o in ((0, ropeA), (1, ropeB)):
                    TT(o[:].rearrange("p (h f) -> p h f", f=FR), proj_ps[:, 0:QK].rearrange("p (h f) -> p h f", f=FR),
                       cs[:, c, b:b + 1].broadcast_to(heads), ALU.mult).then_inc(rope_mul, 1)
                TS(v_sb[:, b], proj_ps[:, QK:QKV], rstd1[:, b:b + 1], None, ALU.mult).then_inc(v_done, 1)
                a = ropeA[:].rearrange("p (h c f) -> p h c f", c=2, f=FR)
                s = ropeB[:].rearrange("p (h c f) -> p h c f", c=2, f=FR)
                dve.wait_ge(rope_mul, 2 * (b + 1))
                if b >= 2:
                    dve.wait_ge(qk_hi_done, 2 * (b - 1))
                    dve.wait_ge(qk_lo_done, 2 * (b - 1))
                TT(qk[:, b % 2, :, 0:FR], a[:, :, 0], s[:, :, 1], ALU.subtract).then_inc(rope_done, 1)
                TT(qk[:, b % 2, :, FR:HD], a[:, :, 1], s[:, :, 0], ALU.add).then_inc(rope_done, 1)

            def stack_low(b):
                dve.wait_ge(rope_done, 2 * (b + 1))
                dve.wait_ge(qk_hi_done, 2 * (b + 1))
                if b >= 2:
                    dve.wait_ge(turned, 2 * (b - 1))
                    dve.wait_ge(kturned, b - 1)
                st = stack[:, b % 2]
                TT(st[:, 0:NH, 1].bitcast(F32R), qk[:, b % 2, 0:NH], st[:, 0:NH, 0],
                   ALU.subtract).then_inc(qk_lo_done, 1)
                TT(st[:, NH, 2].bitcast(F32R), qk[:, b % 2, NH], st[:, NH, 0], ALU.subtract).then_inc(qk_lo_done, 1)

            def maxima(b):
                if b >= 2:
                    dve.wait_ge(st_done, 2 * (b - 1))
                dve.wait_ge(s1_done, 2 * (b + 1))
                for g in range(2):
                    nc.vector.tensor_reduce(top[:, b % 2, HG * g:HG * g + HG],
                                            score_ps[g][:, :].rearrange("p (h t) -> p h t", h=HG),
                                            AX.X, ALU.max).then_inc(top_done, 1)

            def context(b):
                dve.wait_ge(rden_done, b + 1)
                if b >= 2:
                    dve.wait_ge(ctx_hi_done, b - 1)
                    dve.wait_ge(ctx_lo_done, b - 1)
                TT(ctxn[:, b % 2], ctx_ps[:, 0:K * S].rearrange("p (k s) -> p k s", k=K), rden[:],
                   ALU.mult).then_inc(ctxn_done, 1)

            def context_low(b):
                dve.wait_ge(ctx_hi_done, b + 1)
                if b == NB:
                    dve.wait_ge(wo_done, K)
                TT(ctx_lo[:, :, tok(b)], ctxn[:, b % 2], ctx_hi[:, :, tok(b)].bitcast(F32),
                   ALU.subtract).then_inc(ctx_lo_done, 1)

            def x2(n, tiles=range(K)):
                for m in tiles:
                    dve.wait_ge(wo_done, K * n + m + 1)
                    r = res_sb[:, m, half(n)]
                    TT(r, attn_out_ps[n][m][:, :], r, ALU.add).then_inc(x2_done, 1)

            def square_sum(n):
                dve.wait_ge(sq2_done, K * (n + 1))
                TT(sqsum[:], sq[:, 0], sq[:, 1], ALU.add).then_inc(sqsum2_done, 1)

            def normed(n, tiles=range(K)):
                dve.wait_ge(rstd2_done, n + 1)
                dve.wait_ge(gain2_done, K)
                for k in tiles:
                    for j in range(NB):
                        b = NB * n + j
                        STT(hf[:, k, j * S:(j + 1) * S], res_sb[:, k, b * S:(b + 1) * S], gain2[:, k, b:b + 1],
                            rstd[:, j * S:(j + 1) * S], ALU.mult, ALU.mult).then_inc(h_done, 1)

            def normed_low(n):
                if n:
                    dve.wait_ge(up_mm, FT * n)
                for k in range(K):
                    dve.wait_ge(h_hi_done, K * n + k + 1)
                    TT(h_lo[:, k], hf[:, k], h_hi[:, k].bitcast(F32), ALU.subtract).then_inc(h_lo_done, 1)

            def gated(n, f):
                i = FT * n + f
                dve.wait_ge(gate_done, i + 1)
                dve.wait_ge(up_mm, i + 1)
                w = width(n)
                TT(act[:, i % 2, 0:w], gate_up_ps(n, f)[1][:, 0:w], act[:, i % 2, 0:w], ALU.mult).then_inc(act_done, 1)

            def act_low(n, f):
                dve.wait_ge(act_hi_done, FT * n + f + 1)
                dve.wait_ge(act_lo_done, FT * n + f)
                TT(act_lo[:, f, chunk_in_half(n)], act[:, f % 2, 0:width(n)],
                   act_hi[:, f, chunk_in_half(n)].bitcast(F32), ALU.subtract).then_inc(act_lo_done, 1)

            def x3(n, tiles=range(K)):
                for m in tiles:
                    dve.wait_ge(down_done, K * n + m + 1)
                    r = res_sb[:, m, chunk(n)]
                    TT(r, down_ps[m][:, 0:width(n)], r, ALU.add).then_inc(x3_done, 1)

            def x3_low(n, tiles=range(K)):
                for m in tiles:
                    dve.wait_ge(x3_hi_done, K * n + m + 1)
                    TT(x3_lo[:, m, chunk_in_half(n)], res_sb[:, m, chunk(n)],
                       x3_hi[:, m, chunk_in_half(n)].bitcast(F32), ALU.subtract).then_inc(x3_lo_done, 1)

            def row(a, c):
                return a[:, c % 2 * QT:(c % 2 + 1) * QT]

            def expert_out(c):
                dve.wait_ge(e2_done, c + 1)
                if c >= 2:
                    dve.wait_ge(s_done, QS * K * (c - 1))
                    dve.wait_ge(var_done, c - 1)
                y, p = yln[:, c % 2, 0], [expert_out_ps[:, g * QT:(g + 1) * QT] for g in range(K)]
                TS(y[:, 1], p[1], col(C_B2 + 1), None, ALU.add).then_inc(y_done, 1)
                dve.wait_ge(y_done, K * c + 1)
                STT(row(sqsum, c), p[0], col(C_B2), y[:, 1], ALU.add, ALU.add).then_inc(ysum_done, 1)
                TS(y[:, 0], p[0], col(C_B2), None, ALU.add).then_inc(y_done, 1)

            def centred(c):
                dve.wait_ge(mean_done, c + 1)
                if c >= 2:
                    dve.wait_ge(z_done, c - 1)
                dve.wait_ge(y_done, K * (c + 1))
                for k in range(K):
                    TT(yln[:, c % 2, 1, k], yln[:, c % 2, 0, k], mean_ps[:, 0:QT], ALU.subtract).then_inc(dev_done, 1)

            def last_squares():
                c = QUARTERS - 1
                for k in range(K):
                    dve.wait_ge(dev_done, K * c + k + 1)
                    TT(sq4[:, c % 2, k], yln[:, c % 2, 1, k], yln[:, c % 2, 1, k], ALU.mult).then_inc(sqd_done, 1)

            def dev_sum(c):
                dve.wait_ge(sqd_done, K * (c + 1))
                TT(row(sqsum, c), sq4[:, c % 2, 0], sq4[:, c % 2, 1], ALU.add).then_inc(sqdsum_done, 1)

            def standard(c):
                dve.wait_ge(rstdv_done, c + 1)
                dve.wait_ge(dev_done, K * (c + 1))
                TT(yln[:, c % 2, 0], yln[:, c % 2, 1],
                   row(rstd, c).rearrange("p (k t) -> p k t", k=1).broadcast_to([P, K, QT]),
                   ALU.mult).then_inc(z_done, 1)

            def s_low(c):
                if c >= 2:
                    dve.wait_ge(out_mm, K * (c - 1))
                for k in range(K):
                    dve.wait_ge(s_hi_done, K * c + k + 1)
                    TT(s4_lo[:, c % 2, k], s4[:, c % 2, k], s4_hi[:, c % 2, k].bitcast(F32),
                       ALU.subtract).then_inc(s_lo_done, 1)

            def finish(c):
                for m in range(K):
                    dve.wait_ge(out_mm, K * c + (m + 1 if c == QUARTERS - 1 else K))
                    r = res_sb[:, m, quarter(c)]
                    STT(r, last_ps(c, m), col(C_OUTB + m), r, ALU.add, ALU.add).then_inc(fin_done, 1)

            def scale_and_shift():
                dve.wait_ge(emb_done, 2)
                for m in range(2 * K):
                    TS(shiftb[:, m], emb_ps[:, m * B:(m + 1) * B], col(C_EMBB + m), None,
                       ALU.add).then_inc(shift_done, 1)

            def layer_norm_affine():
                dve.wait_ge(shift_done, 2 * K)
                for m in range(K):
                    TS(lnA[:, m], shiftb[:, m], 1.0, col(C_LNG + m), ALU.add, ALU.mult).then_inc(shift_done, 1)
                    TS(lnB[:, m], shiftb[:, m], 1.0, col(C_LNB + m), ALU.add, ALU.mult).then_inc(shift_done, 1)
                dve.wait_ge(shift_done, 4 * K)
                TT(lnB[:], lnB[:], shiftb[:, K:2 * K], ALU.add).then_inc(lnab_done, 3)

            rotary_tables()
            gains(bank[7], C_LN1W, gain1, scale1_done, gain1_done)
            dve.wait_ge(wqkv_split, 1)
            TT(wqkv_lo, wqkv_raw, wqkv_hi.bitcast(F32), ALU.subtract).then_inc(wqkv_split, 1)
            dve.wait_ge(gain1_done, K)
            xg_low(0)
            second_xg_high()
            xg_low(1)
            scaled_table(0)
            rope(0)
            stack_low(0)
            rope(1)
            xg_low(2)
            stack_low(1)
            dve.wait_ge(ld["ident"], 16)
            TS(negid[:], id_sb[:], -1.0, None, ALU.mult).then_inc(negid_ready, 1)
            scaled_table(1)
            maxima(0)
            gains(bank[1], C_LN2W, gain2, scale2_done, gain2_done)
            for b in range(B):
                if b == NB + 3:
                    normed(0, [1])
                if b + 3 < B:
                    xg_low(b + 3)
                if b >= 1:
                    context(b - 1)
                if b == NB + 3:
                    normed_low(0)
                if b == NB:
                    context_low(b - 1)
                if b == NB + 2:
                    normed(0, [0])
                if b in (2, 4):
                    scaled_table(b // 2 + 1)
                if b + 2 < B:
                    rope(b + 2)
                if b == NB:
                    x2(0, [0])
                if b + 1 < B:
                    maxima(b + 1)
                if b == NB:
                    x2(0, [1])
                if b + 2 < B:
                    stack_low(b + 2)
                if b >= 1 and b != NB:
                    context_low(b - 1)
                if b == NB + 1:
                    square_sum(0)
            context(B - 1)
            context_low(B - 1)
            for f in range(FT):
                gated(0, f)
                if f == 3:
                    scale_and_shift()
                    layer_norm_affine()
                if f > POOL_LOWS:
                    act_low(0, f - 1)
                if f == 2:
                    x2(1)
                if f == 4:
                    square_sum(1)
            act_low(0, FT - 1)
            normed(1)
            normed_low(1)
            for m in range(K):
                x3(0, [m])
                x3_low(0, [m])
            expert_out(0)
            gated(1, 0)
            gated(1, 1)
            expert_out(1)
            gated(1, 2)
            centred(0)
            gated(1, 3)
            centred(1)
            gated(1, 4)
            dev_sum(0)
            gated(1, 5)
            dev_sum(1)
            gated(1, 6)
            gated(1, 7)
            act_low(1, 6)
            act_low(1, 7)
            standard(0)
            standard(1)
            x3(1, [0])
            x3_low(1, [0])
            x3(1, [1])
            gated(2, 0)
            x3_low(1, [1])
            s_low(0)
            gated(2, 1)
            finish(0)
            gated(2, 2)
            expert_out(2)
            for f in range(3, FT):
                gated(2, f)
                if f == 4:
                    s_low(1)
                if f == 5:
                    centred(2)
                if f == 7:
                    act_low(2, 6)
                    dev_sum(2)
                    act_low(2, 7)
                    finish(1)
            x3(2, [0])
            x3_low(2, [0])
            standard(2)
            x3(2, [1])
            x3_low(2, [1])
            expert_out(3)
            centred(3)
            last_squares()
            s_low(2)
            standard(3)
            finish(2)
            s_low(3)
            finish(3)

        @block.tensor
        def _(pe):
            MM = nc.tensor.matmul

            def mm3(out_ap, parts, first=True, last=True):
                for i, (lh, ll, rh, rl) in enumerate(parts):
                    MM(out_ap, lh, rh, start=first and i == 0, stop=False)
                    MM(out_ap, lh, rl, start=False, stop=False)
                    mm = MM(out_ap, ll, rh, start=False, stop=last and i == len(parts) - 1)
                return mm

            def scale_of(tw_sb, ps, load, done):
                pe.wait_ge(ld["small"], 16)
                pe.wait_ge(load, 16)
                for m in range(K):
                    for k in range(K):
                        mm = MM(ps[:, m * B:(m + 1) * B], tw_sb[:, k, m * P:(m + 1) * P],
                                small_sb[:, C_COND + k * B:C_COND + (k + 1) * B], start=k == 0, stop=k == K - 1)
                mm.then_inc(done, 1)

            def keep_busy(ps, n):
                for _ in range(n):
                    MM(ps[:, 0:P], filler[:], filler[:], start=True, stop=True)

            def project(b):
                if b == 0:
                    pe.wait_ge(wqkv_split, 2)
                else:
                    pe.wait_ge(rope_mul, 2 * b)
                    pe.wait_ge(v_done, b)
                if b == NB + 3:
                    pe.wait_ge(x2_done, K)
                pe.wait_ge(xg_hi_done, K * (b + 1))
                pe.wait_ge(xg_lo_done, K * (b + 1))
                mm3(proj_ps[:, 0:QKV], [(xg_hi[:, b % 3, k], xg_lo[:, b % 3, k], wqkv_hi[:, k], wqkv_lo[:, k])
                                        for k in range(K)]).then_inc(proj_done, 1)

            def turn_key(b):
                pe.wait_ge(qk_hi_done, 2 * (b + 1))
                pe.wait_ge(qk_lo_done, 2 * (b + 1))
                if b == 0:
                    pe.wait_ge(ld["ident"], 16)
                if b >= 1:
                    pe.wait_ge(top_done, 2 * b)
                nc.tensor.transpose(score_ps[0][0:96, 0:S], stack[:, b % 2, NH].rearrange("p c d -> p (c d)"),
                                    id_sb[:]).then_inc(kturned, 1)

            def turn_queries(b):
                if b == 1:
                    pe.wait_ge(gain1_done, K)
                if b >= 2:
                    pe.wait_ge(exp_done, 2 * (b - 1))
                for g in range(2):
                    for h in range(HG):
                        mm = nc.tensor.transpose(pair(b)[g][0:96, h * S:(h + 1) * S],
                                                 stack[:, b % 2, HG * g + h].rearrange("p c d -> p (c d)"), id_sb[:])
                    mm.then_inc(turned, 1)

            def scores_for_max(b):
                pe.wait_ge(kT_done, b + 1)
                for g in range(2):
                    pe.wait_ge(qT_done, 2 * b + g + 1)
                    for h in range(HG):
                        mm = MM(score_ps[g][:, h * S:(h + 1) * S], qkT[0:96, b % 2, HG * g + h], kT[0:96, b % 2],
                                start=True, stop=True)
                    mm.then_inc(s1_done, 1)

            def scores_transposed(b):
                if b == 0:
                    pe.wait_ge(negid_ready, 1)
                for g in range(2):
                    ps = pair(b)[g]
                    MM(ps[:, :], kT[0:96, b % 2], qkT[0:96, b % 2, HG * g:HG * g + HG].rearrange("p h s -> p (h s)"),
                       start=True, stop=False)
                    pe.wait_ge(top_done, 2 * b + g + 1)
                    for h in range(HG):
                        mm = MM(ps[:, h * S:(h + 1) * S],
                                top[:, b % 2, HG * g + h:HG * g + h + 1].broadcast_to([P, S]), negid[:],
                                start=False, stop=h == HG - 1)
                    mm.then_inc(st_done, 1)

            def weigh_values(b):
                pe.wait_ge(exp_done, 2 * (b + 1))
                pe.wait_ge(v_done, b + 1)
                if b == 0:
                    pe.wait_ge(consts_ready, 2)
                    pe.wait_ge(gain2_done, K)
                if b >= 1:
                    pe.wait_ge(ctxn_done, b)
                if b == NB:
                    pe.wait_ge(x2_done, 1)
                for c, w in ((0, v_sb[:, b]), (1, ones[:])):
                    for r in range(4):
                        mm = MM(ctx_ps[32 * r:32 * r + 32, c * K * S:(c + 1) * K * S], w,
                                prob[:, b % 2, r::4], start=True, stop=True)
                mm.then_inc(pv_done, 1)

            def attn_out(n, m):
                if m == 0:
                    pe.wait_ge(weight_lo, W_WO)
                    pe.wait_ge(ctx_hi_done, NB * (n + 1))
                    pe.wait_ge(ctx_lo_done, NB * (n + 1))
                if n == 0 and m == 0:
                    pe.wait_ge(ctxn_done, NB)
                elif n == 0:
                    pe.wait_ge(rope_mul, 2 * (NB + 3))
                    pe.wait_ge(v_done, NB + 3)
                else:
                    pe.wait_ge(top_done, 2 * B)
                ms = slice(m * P, (m + 1) * P)
                mm3(attn_out_ps[n][m][:, :], [(wo_hi[:, k, ms], wo_lo[:, k, ms], ctx_hi[:, k], ctx_lo[:, k])
                                              for k in range(K)]).then_inc(wo_done, 1)

            def mean_of_squares(n):
                pe.wait_ge(sqsum2_done, n + 1)
                pe.wait_ge(x2_done, K * (n + 1))
                if n == 0:
                    pe.wait_ge(rope_mul, 2 * B)
                    pe.wait_ge(v_done, B)
                MM(ms2_ps[n][:, :], avg[:], sqsum[:], start=True, stop=True).then_inc(ms2_done, 1)

            def gate_or_up(n, f, u):
                i = FT * n + f
                pe.wait_ge(weight_lo, W_GU + f)
                before = last_in_bank(n, f)
                if before:
                    pe.wait_ge(gate_done if n == 0 and u == 0 else act_done, before)
                elif u == 0 and n == 0:
                    pe.wait_ge(exp_done, 2 * (B - 1))
                if GATE_UP_BANK[n][f] == 0:
                    pe.wait_ge(gelu_done, E * (n + 1))
                elif GATE_UP_BANK[n][f] == 1:
                    pe.wait_ge(fin_done, K)
                elif GATE_UP_BANK[n][f] == 4:
                    pe.wait_ge(y_done, K * 2)
                ts = chunk_in_half(n)
                for k in range(K):
                    if f == 0 and u == 0:
                        pe.wait_ge(h_hi_done, K * min(n, 1) + k + 1)
                        pe.wait_ge(h_lo_done, K * min(n, 1) + k + 1)
                    mm = mm3(gate_up_ps(n, f)[u][:, 0:width(n)],
                             [(wgu_hi[:, f, u, k], wgu_lo[:, f, u, k], h_hi[:, k, ts], h_lo[:, k, ts])],
                             first=k == 0, last=k == K - 1)
                mm.then_inc((gate_mm, up_mm)[u], 1)

            def down(n, m):
                if n:
                    pe.wait_ge(gelu_done, E * (n + 1))
                elif m == 0:
                    pe.wait_ge(exp_done, 2 * B)
                ms = slice(m * P, (m + 1) * P)
                for f in range(FT):
                    if m == 0:
                        pe.wait_ge(weight_lo, W_D + f)
                        pe.wait_ge(act_hi_done, FT * n + f + 1)
                        pe.wait_ge(act_lo_done, FT * n + f + 1)
                    mm = mm3(down_ps[m][:, 0:width(n)], [(wd_hi[:, f, ms], wd_lo[:, f, ms],
                                                          act_hi[:, f, chunk_in_half(n)],
                                                          act_lo[:, f, chunk_in_half(n)])],
                             first=f == 0, last=f == FT - 1)
                mm.then_inc(down_done, 1)

            def expert_in(c):
                for e in range(E):
                    k = e // 4
                    n = CHUNK_OF_QUARTER[c]
                    if e % 4 == 0:
                        pe.wait_ge(x3_hi_done, K * n + k + 1)
                        pe.wait_ge(x3_lo_done, K * n + k + 1)
                        pe.wait_ge(weight_lo, W_1 + k)
                    if e == 0 and c == 0:
                        pe.wait_ge(shift_done, 2 * K)
                    if e == 0 and c >= 2:
                        pe.wait_ge(act_done, FT + 6 if c == 2 else len(CHUNKS) * FT)
                    if e in (2, 4):
                        pe.wait_ge(x3_done, K * n + e // 2)
                    if e % 2 == 0 and c:
                        pe.wait_ge(gelu_done, E * (c - 1) + e + 2)
                    if e == 6 and c >= 2:
                        pe.wait_ge(dev_done, K * c)
                    mm = mm3(expert_in_ps[e // 2][:, e % 2 * QT:(e % 2 + 1) * QT],
                             [(w1_hi[:, e], w1_lo[:, e], x3_hi[:, k, quarter_in_half(c)],
                               x3_lo[:, k, quarter_in_half(c)])])
                    if e % 2:
                        mm.then_inc(e1_done, 1)

            def expert_out(c):
                pe.wait_ge(ld["w2"], 16)
                if c >= 2:
                    pe.wait_ge(act_done, 2 * FT + 1)
                if c == QUARTERS - 1:
                    pe.wait_ge(lnv_done, c)
                elif c:
                    pe.wait_ge(y_done, K * c)
                else:
                    pe.wait_ge(ln2_done, 2)
                for g in range(2):
                    pe.wait_ge(gelu_done, E * c + 4 * g + 4)
                    for r in range(4):
                        mm = MM(expert_out_ps[32 * r:32 * r + 32, g * QT:(g + 1) * QT], w2_sb[:, 4 * g + r],
                                hid[4 * g + r][:, c % 2], start=True, stop=True)
                mm.then_inc(e2_done, 1)

            def row(a, c):
                return a[:, c % 2 * QT:(c % 2 + 1) * QT]

            def mean(c):
                pe.wait_ge(ysum_done, c + 1)
                if c:
                    pe.wait_ge(dev_done, K * c)
                pe.wait_ge(gelu_done, E * max(c + 1, 2))
                MM(mean_ps[:, 0:QT], avg[:], row(sqsum, c), start=True, stop=True).then_inc(mean_done, 1)

            def variance(c):
                if c < QUARTERS - 1:
                    pe.wait_ge(sqdsum_done, c + 1)
                if c < 2:
                    pe.wait_ge(ctxn_done, B)
                elif c == 2:
                    pe.wait_ge(y_done, K * (c + 1))
                else:
                    pe.wait_ge(act_done, len(CHUNKS) * FT)
                if c < QUARTERS - 1:
                    mm = MM(row(var_ps[c], c), avg[:], row(sqsum, c), start=True, stop=True)
                else:
                    for k in range(K):
                        pe.wait_ge(sqd_done, K * c + k + 1)
                        mm = MM(row(var_ps[c], c), avg[:], sq4[:, c % 2, k], start=k == 0, stop=k == K - 1)
                mm.then_inc(var_done, 1)

            def last_product(c):
                pe.wait_ge(weight_lo, W_OUT)
                if c < QUARTERS - 1:
                    if c:
                        pe.wait_ge(fin_done, K * c)
                        pe.wait_ge(act_done, 2 * FT + 4)
                    pe.wait_ge(lnv_done, max(c + 1, 2))
                else:
                    pe.wait_ge(act_done, len(CHUNKS) * FT)
                    pe.wait_ge(y_done, K * (c + 1))
                tiles = [(m, k) for m in range(K) for k in range(K)]
                if c == QUARTERS - 1:
                    tiles = [(m, k) for k in range(K) for m in range(K)]
                for m, k in tiles:
                    pe.wait_ge(s_hi_done, K * c + k + 1)
                    pe.wait_ge(s_lo_done, K * c + k + 1)
                    ms = slice(m * P, (m + 1) * P)
                    mm = mm3(last_ps(c, m), [(outw_hi[:, k, ms], outw_lo[:, k, ms], s4_hi[:, c % 2, k],
                                              s4_lo[:, c % 2, k])], first=k == 0, last=k == K - 1)
                    if k == K - 1:
                        mm.then_inc(out_mm, 1)

            def embedding(tiles):
                pe.wait_ge(scond_done, 1)
                pe.wait_ge(ld["embw"], 16)
                pe.wait_ge(ln2_done, 1)
                for m in tiles:
                    for k in range(K):
                        mm = MM(emb_ps[:, m * B:(m + 1) * B], emb_sb[:, k, m * P:(m + 1) * P], scond[:, k],
                                start=k == 0, stop=k == K - 1)
                mm.then_inc(emb_done, 1)

            pe.wait_ge(filler_ready, 1)
            keep_busy(bank[1], 28)
            scale_of(tw1_sb, bank[7], ld["tw1"], scale1_done)
            keep_busy(bank[1], 16)
            project(0)
            project(1)
            keep_busy(bank[1], 30)
            turn_key(0)
            turn_queries(0)
            keep_busy(bank[1], 8)
            scale_of(tw2_sb, bank[1], ld["tw2"], scale2_done)
            scores_for_max(0)
            for b in range(B):
                if b + 2 < B:
                    project(b + 2)
                if b + 1 < B:
                    turn_key(b + 1)
                    turn_queries(b + 1)
                if b == NB + 2:
                    mean_of_squares(0)
                scores_transposed(b)
                if b == NB:
                    attn_out(0, 0)
                if b + 1 < B:
                    scores_for_max(b + 1)
                if b == NB:
                    attn_out(0, 1)
                if b >= B - 2:
                    embedding(range(K) if b == B - 2 else range(K, 2 * K))
                weigh_values(b)
            for f in range(FT):
                gate_or_up(0, f, 0)
                gate_or_up(0, f, 1)
                if f == 1:
                    attn_out(1, 0)
                    attn_out(1, 1)
                if f == 5:
                    mean_of_squares(1)
            down(0, 0)
            down(0, 1)
            gate_or_up(1, 0, 0)
            gate_or_up(1, 0, 1)
            expert_in(0)
            expert_in(1)
            gate_or_up(1, 1, 0)
            gate_or_up(1, 1, 1)
            expert_out(0)
            gate_or_up(1, 2, 0)
            gate_or_up(1, 2, 1)
            expert_out(1)
            for f in range(3, FT):
                gate_or_up(1, f, 0)
                if f == 3:
                    mean(0)
                gate_or_up(1, f, 1)
                if f == 4:
                    mean(1)
                if f in (6, 7):
                    variance(f - 6)
            down(1, 0)
            down(1, 1)
            gate_or_up(2, 0, 0)
            gate_or_up(2, 0, 1)
            gate_or_up(2, 1, 0)
            gate_or_up(2, 1, 1)
            expert_in(2)
            last_product(0)
            gate_or_up(2, 2, 0)
            gate_or_up(2, 2, 1)
            gate_or_up(2, 3, 0)
            gate_or_up(2, 3, 1)
            expert_out(2)
            for f in range(4, FT):
                gate_or_up(2, f, 0)
                gate_or_up(2, f, 1)
                if f == 5:
                    mean(2)
                if f == 7:
                    last_product(1)
            down(2, 0)
            variance(2)
            down(2, 1)
            expert_in(3)
            expert_out(3)
            pe.wait_ge(act_done, len(CHUNKS) * FT)
            keep_busy(bank[3], 12)
            mean(3)
            keep_busy(bank[3], 24)
            variance(3)
            last_product(2)
            pe.wait_ge(gelu_done, E * QUARTERS)
            keep_busy(bank[0], 36)
            last_product(3)


def kernel(x, pos_BxS, cond_2048, L0_cond_ln1_w, L0_cond_ln1_tw, L0_cond_ln2_w, L0_cond_ln2_tw, L0_cond_Wq,
           L0_cond_Wk, L0_cond_Wv, L0_cond_Wo, L0_cond_Wg, L0_cond_Wu, L0_cond_Wd, L1_cond_W1, L1_cond_b1,
           L1_cond_W2, L1_cond_b2, L1_cond_emb_W, L1_cond_emb_b, L1_cond_ln_g, L1_cond_ln_b, L1_cond_out_W,
           L1_cond_out_b):
    import numpy as np
    import concourse.bacc as bacc
    from concourse.bass_utils import run_bass_kernel_spmd

    def tiles(a, axis=0):
        a = np.asarray(a)
        return a.reshape(a.shape[0] // P, P, -1).transpose(1, 0, 2)

    def turned(w):
        return tiles(np.asarray(w).T)

    x = np.asarray(x)
    inv_freq = (np.float32(1.0) / np.float32(10000.0) ** (np.arange(0, HD, 2, dtype=np.float32) / np.float32(HD)))
    small = np.concatenate(
        [np.asarray(a).reshape(-1, P).T for a in (L0_cond_ln1_w, L0_cond_ln2_w, L1_cond_ln_g, L1_cond_ln_b,
                                                  L1_cond_out_b, L1_cond_b2, L1_cond_emb_b, L1_cond_b1)]
        + [tiles(np.asarray(cond_2048).T).reshape(P, K * B), np.tile(inv_freq.astype(np.float32), (P, 1))], axis=1)
    wg, wu = (np.asarray(w).reshape(FT, P, K, P) for w in (L0_cond_Wg, L0_cond_Wu))
    arrays = {
        "xT": tiles(x.reshape(T, H).T),
        "xn": x.transpose(1, 0, 2),
        "small": small,
        "posT": np.asarray(pos_BxS).T,
        "ident": np.eye(P, dtype=np.float32),
        "tw1": turned(L0_cond_ln1_tw),
        "tw2": turned(L0_cond_ln2_tw),
        "wqkv": turned(np.concatenate([np.asarray(w) for w in (L0_cond_Wq, L0_cond_Wk, L0_cond_Wv)])),
        "wo": turned(L0_cond_Wo),
        "wgu": np.stack([wg, wu], axis=1).transpose(4, 0, 1, 3, 2),
        "wd": turned(L0_cond_Wd),
        "w1": np.asarray(L1_cond_W1).transpose(1, 0, 2),
        "w2": np.asarray(L1_cond_W2).transpose(1, 0, 2),
        "embw": tiles(L1_cond_emb_W),
        "outw": tiles(L1_cond_out_W),
    }
    nc = bacc.Bacc("TRN2", target_bir_lowering=False, num_devices=1)
    feed, args = {}, []
    for name, a in arrays.items():
        a = np.ascontiguousarray(a)
        feed[f"in_{name}"] = a
        args.append(nc.dram_tensor(f"in_{name}", a.shape, mybir.dt.from_np(a.dtype), kind="ExternalInput").ap())
    args.append(nc.dram_tensor("out_yT", (P, K, T), F32, kind="ExternalOutput").ap())
    cond_block_kernel(nc, *args)
    r = run_bass_kernel_spmd(nc, [feed], core_ids=[0])
    yT = r.results[0]["out_yT"]
    return yT.transpose(1, 0, 2).reshape(H, T).T.reshape(B, S, H)
```
